# Optimizing a Trainium2 kernel written in Bass

```python
import numpy as np
import jax
import jax.numpy as jnp

def _softmax(x, axis=-1):
    return jax.nn.softmax(x, axis=axis)

def _gelu(x):
    return jax.nn.gelu(x, approximate=True)

def _silu(x):
    return jax.nn.silu(x)

def _sigmoid(x):
    return jax.nn.sigmoid(x)

def _layernorm(x, axis=-1, eps=1e-05):
    m = jnp.mean(x, axis=axis, keepdims=True)
    v = jnp.var(x, axis=axis, keepdims=True)
    return (x - m) / jnp.sqrt(v + eps)

def _scatter_add(tgt, idx, src, axis=0):
    return tgt.at[idx].add(src)

def _segment_sum(src, seg, n):
    return jax.ops.segment_sum(src, seg, n)
kernel_name = 'mk_gnn_preln_d4_gnn_r8_113cc4'

def setup_inputs(seed: int=0):
    np.random.seed(seed)
    _w = jnp.asarray

    def _rec_inputs():
        import jax
        import jax.numpy as jnp
        _gk = jax.random.key(seed)
        x = -0.000202 + 1 * jax.random.normal(jax.random.fold_in(_gk, 1), (12500, 64), jnp.float32)
        src = jax.random.randint(jax.random.fold_in(_gk, 2), (400000,), 0, 12500, jnp.int32)
        dst = jnp.minimum((12500 * jax.random.uniform(jax.random.fold_in(_gk, 3), (400000,)) ** 2.0).astype(jnp.int32), 99999)
        _o = jnp.argsort(dst, stable=True)
        src = src[_o]
        dst = dst[_o]
        edge_weight = jax.random.uniform(jax.random.fold_in(_gk, 13), (400000,), jnp.float32, 0.0, 0.999999)
        return (x, src, dst, edge_weight)
    x, src, dst, edge_weight = _rec_inputs()

    def _L0_gnn_setup():
        import jax, jax.numpy as jnp
        import numpy as np
        N_NODES = 12500
        N_EDGES = 200000
        IN_CH = 64
        OUT_CH = 64
        key = jax.random.key(seed)
        ks = jax.random.split(key, 6)
        x = jax.random.normal(ks[0], (N_NODES, IN_CH), dtype=jnp.float32)
        edge_index = jax.random.randint(ks[1], (2, N_EDGES), 0, N_NODES, dtype=jnp.int64)
        W1 = jax.random.normal(ks[2], (2 * IN_CH, OUT_CH), dtype=jnp.float32) * (1.0 / np.sqrt(2 * IN_CH))
        b1 = jnp.zeros((OUT_CH,), dtype=jnp.float32)
        W2 = jax.random.normal(ks[3], (OUT_CH, OUT_CH), dtype=jnp.float32) * (1.0 / np.sqrt(OUT_CH))
        b2 = jnp.zeros((OUT_CH,), dtype=jnp.float32)
        return {'x': x, 'edge_index': edge_index, 'W1': W1, 'b1': b1, 'W2': W2, 'b2': b2}
    _L0_gnn_all = _L0_gnn_setup()
    _L0_gnn_in = {k: v for k, v in _L0_gnn_all.items() if k in ('W1', 'b1', 'W2', 'b2')}
    del _L0_gnn_all

    def _L1_gnn_setup():
        import jax, jax.numpy as jnp
        import numpy as np
        N_NODES = 12500
        N_EDGES = 200000
        D_IN = 64
        D_OUT = 64
        key = jax.random.key(seed)
        k1, k2, k3, k4 = jax.random.split(key, 4)
        x = jax.random.normal(k1, (N_NODES, D_IN), dtype=jnp.float32)
        src = jax.random.randint(k2, (N_EDGES,), 0, N_NODES, dtype=jnp.int32)
        dst = jax.random.randint(k3, (N_EDGES,), 0, N_NODES, dtype=jnp.int32)
        W = jax.random.normal(k4, (D_IN, D_OUT), dtype=jnp.float32) / np.float32(np.sqrt(D_IN))
        b = jnp.zeros((D_OUT,), dtype=jnp.float32)
        return {'x': x, 'src': src, 'dst': dst, 'W': W, 'b': b}
    _L1_gnn_all = _L1_gnn_setup()
    _L1_gnn_in = {k: v for k, v in _L1_gnn_all.items() if k in ('W', 'b')}
    del _L1_gnn_all

    def _L2_gnn_setup():
        import jax, jax.numpy as jnp
        import numpy as np
        N = 12500
        DEG = 16
        E = N * DEG
        IN_F, H_F, OUT_F = (64, 64, 64)

        def _spmm_mean(h, src, dst, n_nodes):
            deg = jax.ops.segment_sum(jnp.ones_like(src, dtype=h.dtype), dst, num_segments=n_nodes)
            w = (1.0 / jnp.maximum(deg, 1.0))[dst]
            return jax.ops.segment_sum(h[src] * w[:, None], dst, num_segments=n_nodes)
        key = jax.random.key(seed)
        k1, k2, k3, k4, k5, k6 = jax.random.split(key, 6)
        x = jax.random.normal(k1, (N, IN_F), dtype=jnp.float32)
        dst = jnp.repeat(jnp.arange(N, dtype=jnp.int32), DEG)
        src = jax.random.randint(k2, (E,), 0, N, dtype=jnp.int32)
        s1 = 1.0 / np.sqrt(2 * IN_F)
        s2 = 1.0 / np.sqrt(2 * H_F)
        W1 = jax.random.uniform(k3, (2 * IN_F, H_F), jnp.float32, -s1, s1)
        b1 = jax.random.uniform(k4, (H_F,), jnp.float32, -s1, s1)
        W2 = jax.random.uniform(k5, (2 * H_F, OUT_F), jnp.float32, -s2, s2)
        b2 = jax.random.uniform(k6, (OUT_F,), jnp.float32, -s2, s2)
        return {'x': x, 'W1': W1, 'b1': b1, 'W2': W2, 'b2': b2, 'src': src, 'dst': dst}
    _L2_gnn_all = _L2_gnn_setup()
    _L2_gnn_in = {k: v for k, v in _L2_gnn_all.items() if k in ('W1', 'b1', 'W2', 'b2')}
    del _L2_gnn_all

    def _L3_gnn_setup():
        import jax, jax.numpy as jnp
        import numpy as np
        key = jax.random.key(seed)
        k1, k2, k3, k4, k5 = jax.random.split(key, 5)
        N, E, C_in, C_out = (12500, 200000, 64, 64)
        x = jax.random.normal(k1, (N, C_in), dtype=jnp.float32)
        edge_index = jax.random.randint(k2, (2, E), 0, N, dtype=jnp.int64)
        edge_weight = jax.random.uniform(k3, (E,), dtype=jnp.float32)
        bound = float(np.sqrt(6.0 / (C_in + C_out)))
        W_self = jax.random.uniform(k4, (C_out, C_in), dtype=jnp.float32, minval=-bound, maxval=bound)
        W_neigh = jax.random.uniform(k5, (C_out, C_in), dtype=jnp.float32, minval=-bound, maxval=bound)
        b_self = jnp.zeros((C_out,), dtype=jnp.float32)
        b_neigh = jnp.zeros((C_out,), dtype=jnp.float32)
        return {'x': x, 'edge_index': edge_index, 'edge_weight': edge_weight, 'W_self': W_self, 'b_self': b_self, 'W_neigh': W_neigh, 'b_neigh': b_neigh, 'num_nodes': N}
    _L3_gnn_all = _L3_gnn_setup()
    _L3_gnn_in = {k: v for k, v in _L3_gnn_all.items() if k in ('W_self', 'b_self', 'W_neigh', 'b_neigh')}
    del _L3_gnn_all
    return {'x': x, 'src': src, 'dst': dst, 'edge_weight': edge_weight, 'L0_gnn_W1': _L0_gnn_in['W1'], 'L0_gnn_b1': _L0_gnn_in['b1'], 'L0_gnn_W2': _L0_gnn_in['W2'], 'L0_gnn_b2': _L0_gnn_in['b2'], 'L1_gnn_W': _L1_gnn_in['W'], 'L1_gnn_b': _L1_gnn_in['b'], 'L2_gnn_W1': _L2_gnn_in['W1'], 'L2_gnn_b1': _L2_gnn_in['b1'], 'L2_gnn_W2': _L2_gnn_in['W2'], 'L2_gnn_b2': _L2_gnn_in['b2'], 'L3_gnn_W_self': _L3_gnn_in['W_self'], 'L3_gnn_b_self': _L3_gnn_in['b_self'], 'L3_gnn_W_neigh': _L3_gnn_in['W_neigh'], 'L3_gnn_b_neigh': _L3_gnn_in['b_neigh']}

def reference(x, src, dst, edge_weight, L0_gnn_W1, L0_gnn_b1, L0_gnn_W2, L0_gnn_b2, L1_gnn_W, L1_gnn_b, L2_gnn_W1, L2_gnn_b1, L2_gnn_W2, L2_gnn_b2, L3_gnn_W_self, L3_gnn_b_self, L3_gnn_W_neigh, L3_gnn_b_neigh):
    import jax
    import jax.numpy as jnp

    def _L0_gnn_ref(x, edge_index, W1, b1, W2, b2):
        import jax, jax.numpy as jnp
        import numpy as np
        N_NODES = 12500
        N_EDGES = 200000
        IN_CH = 64
        OUT_CH = 64
        src = edge_index[0]
        dst = edge_index[1]
        x_i = x[dst]
        x_j = x[src]
        edge_features = jnp.concatenate([x_i, x_j - x_i], axis=-1)
        h = jax.nn.relu(edge_features @ W1 + b1)
        edge_messages = h @ W2 + b2
        out = jax.ops.segment_max(edge_messages, dst, num_segments=x.shape[0])
        return jnp.where(jnp.isfinite(out), out, jnp.zeros_like(out))

    def _L1_gnn_ref(x, src, dst, W, b):
        import jax, jax.numpy as jnp
        import numpy as np
        N_NODES = 12500
        N_EDGES = 200000
        D_IN = 64
        D_OUT = 64
        n = x.shape[0]
        ones = jnp.ones(src.shape, dtype=x.dtype)
        out_deg = jax.ops.segment_sum(ones, src, num_segments=n)
        in_deg = jax.ops.segment_sum(ones, dst, num_segments=n)
        norm_src = jax.lax.rsqrt(jnp.maximum(out_deg, 1.0))
        norm_dst = jax.lax.rsqrt(jnp.maximum(in_deg, 1.0))
        msg = (x * norm_src[:, None])[src]
        agg = jax.ops.segment_sum(msg, dst, num_segments=n) * norm_dst[:, None]
        h = agg @ W + b
        return jax.nn.leaky_relu(h, negative_slope=0.01)

    def _L2_gnn_ref(x, W1, b1, W2, b2, src, dst):
        import jax, jax.numpy as jnp
        import numpy as np
        N = 12500
        DEG = 16
        E = N * DEG
        IN_F, H_F, OUT_F = (64, 64, 64)

        def _spmm_mean(h, src, dst, n_nodes):
            deg = jax.ops.segment_sum(jnp.ones_like(src, dtype=h.dtype), dst, num_segments=n_nodes)
            w = (1.0 / jnp.maximum(deg, 1.0))[dst]
            return jax.ops.segment_sum(h[src] * w[:, None], dst, num_segments=n_nodes)
        n = x.shape[0]
        h_neigh = _spmm_mean(x, src, dst, n)
        h = jnp.concatenate([x, h_neigh], axis=1)
        h = jax.nn.relu(h @ W1 + b1)
        h_neigh2 = _spmm_mean(h, src, dst, n)
        h2 = jnp.concatenate([h, h_neigh2], axis=1)
        return h2 @ W2 + b2

    def _L3_gnn_ref(x, edge_index, edge_weight, W_self, b_self, W_neigh, b_neigh, num_nodes):
        import jax, jax.numpy as jnp
        import numpy as np
        row, col = (edge_index[0], edge_index[1])
        message = x[col] * edge_weight[:, None]
        neigh_agg = jax.ops.segment_sum(message, row, num_segments=num_nodes)
        return x @ W_self.T + b_self + neigh_agg @ W_neigh.T + b_neigh
    edge_index = jnp.stack([src, dst])
    h = jnp.maximum(_layernorm(x, axis=-1), 0.0)
    x = x + _L0_gnn_ref(h, edge_index, L0_gnn_W1, L0_gnn_b1, L0_gnn_W2, L0_gnn_b2)
    h = jnp.maximum(_layernorm(x, axis=-1), 0.0)
    x = x + _L1_gnn_ref(h, src, dst, L1_gnn_W, L1_gnn_b)
    h = jnp.maximum(_layernorm(x, axis=-1), 0.0)
    x = x + _L2_gnn_ref(h, L2_gnn_W1, L2_gnn_b1, L2_gnn_W2, L2_gnn_b2, src, dst)
    h = jnp.maximum(_layernorm(x, axis=-1), 0.0)
    x = x + _L3_gnn_ref(h, edge_index, edge_weight, L3_gnn_W_self, L3_gnn_b_self, L3_gnn_W_neigh, L3_gnn_b_neigh, 12500)
    return x

_drawn_inputs = setup_inputs


def setup_inputs(seed=0):
    import zlib

    import numpy as np

    out = dict(_drawn_inputs(seed))
    spreads = {'L0_gnn_b1': (0.0, 0.1),
     'L0_gnn_b2': (0.0, 0.1),
     'L1_gnn_b': (0.0, 0.1),
     'L3_gnn_b_self': (0.0, 0.708),
     'L3_gnn_b_neigh': (0.0, 0.668)}
    factors = {'L2_gnn_b1': 2.732}
    for name, (base, spread) in spreads.items():
        noise = np.random.default_rng([zlib.crc32(name.encode()), seed]).standard_normal(out[name].shape)
        drawn = base * np.exp(spread * noise) if base else spread * noise
        out[name] = jnp.asarray(drawn.astype(out[name].dtype))
    for name, factor in factors.items():
        out[name] = (out[name] * factor).astype(out[name].dtype)
    return out
```

```python
import concourse.bass as bass
from concourse import mybir
from contextlib import ExitStack

N, E, D = 12500, 400000, 64
P = 128
TILES = -(-N // P)
ROWS = P * TILES
LANE = E // P
K = 25
R = 5
BLOCKS = LANE // K
ITERS = BLOCKS // R
HG = 5
HBUF = 5
HCOLS = 125
ACC_SETS, ACC_PER_SET = 2, 5
FULL = 3.4028234663852886e38
LAST_ROWS = N - (P - 1) * TILES
BEYOND = 2.0 * E


def build(nc, x, src, dst, edge_weight, l0_w1, l0_b1, l0_w2, l0_b2, l1_w, l1_b,
          l2_w1, l2_b1, l2_w2, l2_b2, l3_ws, l3_bs, l3_wn, l3_bn, out):
    f32, bf16, i32 = mybir.dt.float32, mybir.dt.bfloat16, mybir.dt.int32
    ALU, ACT, AX = mybir.AluOpType, mybir.ActivationFunctionType, mybir.AxisListType
    assert N <= ROWS and E == P * LANE and LANE == K * R * ITERS and BLOCKS == R * ITERS
    ctx = ExitStack()
    with ctx:
        def sb(name, shape, dt=f32):
            return ctx.enter_context(nc.sbuf_tensor(name, shape, dt))

        def ps(name, shape):
            return ctx.enter_context(nc.psum_tensor(name, shape, f32))

        sems = {}

        def sem(name):
            if name not in sems:
                sems[name] = ctx.enter_context(nc.semaphore(name))
            return sems[name]

        def dram(name, shape, dt=f32):
            return nc.dram_tensor(name, shape, dt).ap()

        tab_edge_a = dram("tab_edge_a", (ROWS, D))
        tab_edge_b = dram("tab_edge_b", (ROWS, D))
        tab_gcn = dram("tab_gcn", (ROWS, D))
        tab_hop1 = dram("tab_hop1", (ROWS, D))
        tab_hop2 = dram("tab_hop2", (ROWS, D))
        tab_last = dram("tab_last", (ROWS, D))
        edge_rows = dram("edge_rows", (E, D))
        first_rows = dram("first_rows", (E, D))
        accs = [dram(f"acc{k}", (ROWS + P, D)) for k in range(ACC_SETS * ACC_PER_SET)]

        X = sb("X", [P, TILES, D])
        HM = sb("HM", [P, TILES, 2 * D])
        H, M = HM[:, :, 0:D], HM[:, :, D:2 * D]
        dst_f = sb("dst_f", [P, LANE])
        limit = dst_f
        keep = sb("keep", [P, LANE])
        ring = sb("ring", [P, R, K, D])
        fill = sb("fill", [P, R, K, D])
        idx = sb("idx", [P, R, K], i32)
        idx2 = sb("idx2", [P, R, K], i32)
        wblk = sb("wblk", [P, R, K])
        mblk = sb("mblk", [P, 2, K])
        srcf = sb("srcf", [P, K])
        dupc = sb("dupc", [P, K])
        dup1 = sb("dup1", [P, K])
        dup2 = sb("dup2", [P, K])
        dupjunk = sb("dupjunk", [P, 2, 4, P], bf16)
        hT = sb("hT", [P, 2, 512])
        eqw = sb("eqw", [P, 2, 4, P])
        oh_q = sb("oh_q", [P, HBUF, HG, P], bf16)
        oh_r = sb("oh_r", [P, HBUF, HG, TILES], bf16)
        hq, hr, ht = (sb(n, [P, HCOLS]) for n in ("hq", "hr", "ht"))
        hi = sb("hi", [P, HCOLS], i32)
        ident = sb("ident", [P, P])
        before = sb("before", [P, P])
        earlier = sb("earlier", [P, P])
        iota_i = sb("iota_i", [P, P], i32)
        iota_b = sb("iota_b", [P, P], bf16)
        colp_i = sb("colp_i", [P, 2], i32)
        lane0 = sb("lane0", [P, 1])
        spare = sb("spare", [P, 1])
        ones = sb("ones", [P, TILES])
        w_ab = sb("w_ab", [D, 2 * D])
        w_diag = sb("w_diag", [P, P])
        w_gcn = sb("w_gcn", [D, D])
        w_hop1 = sb("w_hop1", [P, D])
        w_hop2 = sb("w_hop2", [P, D])
        w_lastT = sb("w_lastT", [D, 2 * D])
        w_last = sb("w_last", [P, D])
        bias = {n: sb("bias_" + n, [P, D]) for n in ("e1", "e2", "gcn", "hop1", "hop2", "last", "last2")}
        stat = {n: sb("stat_" + n, [P, TILES]) for n in
                ("mean", "var", "rstd", "deg", "has", "incl", "nsrc", "ndst", "inv", "tmp")}
        eps = sb("eps", [P, 1])
        start_i = sb("start_i", [P, TILES], i32)
        end_i = sb("end_i", [P, TILES], i32)
        fix_i = sb("fix_i", [P, 1], i32)
        first_i = sb("first_i", [P, 1], i32)
        prev_i = sb("prev_i", [P, 1], i32)
        col = {n: sb("col_" + n, [P, 1]) for n in
               ("first", "prev", "cnt", "cont", "whole", "k", "contL", "offs", "tot")}
        krow = sb("krow", [D, P])
        krowL = sb("krowL", [D, P])
        carryT = sb("carryT", [D, P + 1])
        tail = sb("tail", [P, D])
        fixrow = sb("fixrow", [P, D])
        lane_init = sb("lane_init", [P, D])

        tp = [ps(f"tp{k}", [P, 512]) for k in range(2)]
        om = [ps(f"om{k}", [P, 512]) for k in range(2)]
        hist = ps("hist", [P, TILES])
        pa = ps("pa", [P, P])
        pb = ps("pb", [P, P])

        lanes = lambda a: a.rearrange("(p c) -> p c", p=P)
        lrows = lambda a: a.rearrange("(p c) f -> p c f", p=P)
        nrows = lambda a: a.rearrange("(p t) f -> p t f", p=P)
        src_l, dst_l, w_l = lanes(src), lanes(dst), lanes(edge_weight)
        flat = lambda a: a.rearrange("p a b -> p (a b)")
        brow = lambda b: b.rearrange("(a n) -> a n", a=1).partition_broadcast(P)

        def wait(e, name, n):
            if not (isinstance(n, int) and n <= 0):
                e.wait_ge(sem(name), n)

        def gate(e):
            e.sem_inc(sem("gate_" + e.engine.name), 1)

        def loop(e, body):
            body(0)
            with e.Fori(1, ITERS) as i:
                body(i)

        class Chain:
            def __init__(self, e, name):
                self.e, self.name, self.n = e, name, 0

            def __call__(self, ins):
                self.n += 1
                ins.then_inc(sem(self.name), 1)
                self.e.wait_ge(sem(self.name), self.n)

            def clear(self):
                self.e.sem_clear(sem(self.name))
                self.n = 0

        def bcast(ap2, n=D):
            return ap2.unsqueeze(2).broadcast_to([P, ap2.shape[1], n])

        def brow3(b, n):
            return b.unsqueeze(1).broadcast_to([P, n, D])

        MM = {}
        NGRP = -(-TILES // 4)

        def mm_base(name):
            return MM.setdefault(name, len(MM)) * NGRP

        for n_ in ("ab", "gcn", "hop1", "hop2", "last"):
            mm_base(n_)

        def mm_tensor(e, name, c0, c1, rhs, m):
            b = mm_base(name)
            kd = c1 - c0
            for g in range(NGRP):
                ts_ = range(4 * g, min(4 * g + 4, TILES))
                wait(e, "mm_copied", b + g - 1)
                for k, t in enumerate(ts_):
                    last = e.transpose(tp[g % 2][0:kd, k * P:(k + 1) * P], HM[:, t, c0:c1], ident[:, :])
                last.then_inc(sem("mm_turned"), 1)
                wait(e, "mm_copied", b + g + 1)
                wait(e, "mm_taken", b + g - 1)
                for k, t in enumerate(ts_):
                    last = e.matmul(om[g % 2][:, k * m:(k + 1) * m], hT[0:kd, g % 2, k * P:(k + 1) * P],
                                    rhs, start=True, stop=True)
                last.then_inc(sem("mm_done"), 1)

        def mm_scalar(e, name, kd):
            b = mm_base(name)
            for g in range(NGRP):
                n = min(4, TILES - 4 * g)
                wait(e, "mm_turned", b + g + 1)
                wait(e, "mm_done", b + g - 1)
                e.activation(hT[0:kd, g % 2, 0:n * P], tp[g % 2][0:kd, 0:n * P], ACT.Copy)\
                    .then_inc(sem("mm_copied"), 1)

        def mm_vector(e, chain, name, m, take):
            b = mm_base(name)
            for g in range(NGRP):
                n = min(4, TILES - 4 * g)
                wait(e, "mm_done", b + g + 1)
                take(om[g % 2][:, 0:n * m].rearrange("p (n m) -> p n m", n=n), 4 * g, n)\
                    .then_inc(sem("mm_taken"), 1)
            e.wait_ge(sem("mm_taken"), b + NGRP)

        def norm_vector(e, chain, l):
            chain(e.tensor_reduce(out=stat["mean"][:, :], in_=X[:, :, :], op=ALU.add, axis=AX.X))
            chain(e.tensor_scalar(stat["mean"][:, :], stat["mean"][:, :], 1.0 / D, None, ALU.mult))
            chain(e.tensor_tensor(H, X[:, :, :], bcast(stat["mean"][:, :]), ALU.subtract))
            chain(e.tensor_tensor(M, H, H, ALU.mult))
            e.tensor_reduce(out=stat["var"][:, :], in_=M, op=ALU.add, axis=AX.X).then_inc(sem("var"), 1)
            e.wait_ge(sem("std"), l + 1)
            chain(e.reciprocal(stat["rstd"][:, :], stat["tmp"][:, :]))
            chain(e.scalar_tensor_tensor(out=H, in0=H, scalar=0.0, in1=bcast(stat["rstd"][:, :]),
                                         op0=ALU.max, op1=ALU.mult))

        def norm_scalar(e, l):
            e.wait_ge(sem("var"), l + 1)
            e.activation(stat["tmp"][:, :], stat["var"][:, :], ACT.Sqrt, bias=eps[:, 0:1], scale=1.0 / D)\
                .then_inc(sem("std"), 1)

        def divide(e, chain, val, n):
            q, r, t, ti = hq[:, 0:n], hr[:, 0:n], ht[:, 0:n], hi[:, 0:n]
            chain(e.tensor_scalar(ti, val, 1.0 / TILES, None, ALU.mult))
            chain(e.tensor_copy(q, ti))
            chain(e.scalar_tensor_tensor(out=r, in0=q, scalar=-float(TILES), in1=val, op0=ALU.mult, op1=ALU.add))
            chain(e.tensor_scalar(t, r, 0.0, None, ALU.is_lt))
            chain(e.tensor_tensor(q, q, t, ALU.subtract))
            chain(e.scalar_tensor_tensor(out=r, in0=t, scalar=float(TILES), in1=r, op0=ALU.mult, op1=ALU.add))
            chain(e.tensor_scalar(t, r, float(TILES), None, ALU.is_ge))
            chain(e.tensor_tensor(q, q, t, ALU.add))
            chain(e.scalar_tensor_tensor(out=r, in0=t, scalar=-float(TILES), in1=r, op0=ALU.mult, op1=ALU.add))

        def onehots(e, name, base, groups):
            for g in range(groups):
                k = g % HBUF
                wait(e, name + "_used", base + g - HBUF + 1)
                for c in range(HG):
                    j = g * HG + c
                    e.tensor_scalar(oh_q[:, k, c, :], iota_b[:, :], hq[:, j:j + 1], None, ALU.is_equal)
                    last = e.tensor_scalar(oh_r[:, k, c, :], iota_b[:, 0:TILES], hr[:, j:j + 1], None, ALU.is_equal)
                last.then_inc(sem(name + "_made"), 1)

        def count_tensor(e, name, base, groups, first):
            for g in range(groups):
                k = g % HBUF
                wait(e, name + "_made", base + g + 1)
                for c in range(HG):
                    last = e.matmul(hist[:, :], oh_q[:, k, c, :], oh_r[:, k, c, :],
                                    start=first and g == 0 and c == 0, stop=c == HG - 1,
                                    skip_group_check=True)
                last.then_inc(sem(name + "_used"), 1)

        HGRP = HCOLS // HG
        HITERS = LANE // HCOLS

        def gather_slot(e, l, i, r, table):
            wait(e, "scanned", i * R + (l * BLOCKS + r - R + 2))
            wait(e, f"stored{r}", i * 16 + l * 16 * ITERS)
            wait(e, f"indexed{r}", i * 16 + (l * 16 * ITERS + 16))
            gate(e)
            for j in range(K):
                e.indirect_dma_start(out=ring[:, r, j, :], out_offset=None, in_=table[:, :],
                                     in_offset=bass.IndirectOffsetOnAxis(ap=idx[:, r, j:j + 1], axis=0))\
                    .then_inc(sem(f"gathered{l}_{r}"), 16)

        def pass_index(e, l, i, r):
            wait(e, f"gathered{l}_{r}", i * (16 * K))
            if l == 0:
                gate(e)
                wait(e, "scanned", i * R + (r - R + 1))
            gate(e)
            e.dma_start(idx[:, r, :], src_l[:, bass.ds((i * R + r) * K, K)]).then_inc(sem(f"indexed{r}"), 16)

        def pass_store(e, l, i, r):
            wait(e, "scanned", i * R + (l * BLOCKS + r + 1))
            e.dma_start(lrows(edge_rows)[:, bass.ds((i * R + r) * K, K), :], ring[:, r, :, :])\
                .then_inc(sem(f"stored{r}"), 16)

        def load_masks(e, chain, i, r):
            chain(e.tensor_copy(mblk[:, 0, :], keep[:, bass.ds((i * R + r) * K, K)]))

        def scan_columns(e, chain, buf, r, mask, op0, op1, cols, other=None):
            for n, j in enumerate(cols):
                prev = buf[:, r, j - 1, :] if j else buf[:, (r - 1) % R, K - 1, :]
                this = buf[:, r, j, :] if other is None else other[:, n * D:(n + 1) * D]
                chain(e.scalar_tensor_tensor(out=buf[:, r, j, :], in0=prev, scalar=mask[:, j:j + 1],
                                             in1=this, op0=op0, op1=op1))

        def sum_pass_vector(e, l):
            chain = Chain(e, "v_loop")

            def body(i):
                for r in range(R):
                    load_masks(e, chain, i, r)
                    wait(e, f"gathered{l}_{r}", i * (16 * K) + 16 * K)
                    scan_columns(e, chain, ring, r, mblk[:, 0, :], ALU.mult, ALU.add, range(K))
                    chain.clear()
                    e.sem_inc(sem("scanned"), 1)
            loop(e, body)

        def fix_tensor(e, l):
            e.wait_ge(sem("tailed"), l + 1)
            e.transpose(pa[0:D, 0:P], tail[:, :], ident[:, :]).then_inc(sem("tail_turned"), 1)
            e.wait_ge(sem("carried"), l + 1)
            e.transpose(pb[:, 0:D], carryT[:, 0:P], ident[0:D, 0:D]).then_inc(sem("carry_turned"), 1)

        def fix_vector(e, chain, l, op0, op1, row, colc):
            e.tensor_copy(tail[:, :], ring[:, R - 1, K - 1, :]).then_inc(sem("tailed"), 1)
            chain(e.memset(M, 0.0))
            e.sem_inc(sem("cleared"), 1)
            e.wait_ge(sem("tail_turned"), l + 1)
            e.tensor_tensor_scan(out=carryT[:, 1:P + 1], data0=row[:, :], data1=pa[0:D, 0:P], initial=0.0,
                                 op0=op0, op1=op1).then_inc(sem("carried"), 1)
            e.wait_ge(sem("carry_turned"), l + 1)
            e.wait_ge(sem("fix_read"), 16 * (l + 1))
            e.scalar_tensor_tensor(out=fixrow[:, :], in0=pb[:, 0:D], scalar=colc[:, 0:1], in1=fixrow[:, :],
                                   op0=op0, op1=op1).then_inc(sem("fix_made"), 1)

        def fix_gpsimd(e, l):
            for r in range(R):
                e.wait_ge(sem(f"stored{r}"), 16 * ITERS * (l + 1))
            e.indirect_dma_start(out=fixrow[:, :], out_offset=None, in_=edge_rows[:, :],
                                 in_offset=bass.IndirectOffsetOnAxis(ap=fix_i[:, 0:1], axis=0))\
                .then_inc(sem("fix_read"), 16)
            e.wait_ge(sem("fix_made"), l + 1)
            e.indirect_dma_start(out=edge_rows[:, :], out_offset=bass.IndirectOffsetOnAxis(ap=fix_i[:, 0:1], axis=0),
                                 in_=fixrow[:, :], in_offset=None).then_inc(sem("fix_written"), 16)
            e.wait_ge(sem("fix_written"), 16 * (l + 1))
            e.wait_ge(sem("cleared"), l + 1)
            for t in range(TILES):
                e.indirect_dma_start(out=M[:, t, :], out_offset=None, in_=edge_rows[:, :],
                                     in_offset=bass.IndirectOffsetOnAxis(ap=end_i[:, t:t + 1], axis=0),
                                     bounds_check=E - 1, oob_is_err=False).then_inc(sem(f"node_rows{l}"), 16)

        def first_rows_gpsimd(e, k, table):
            for t in range(TILES):
                e.indirect_dma_start(out=first_rows[:, :],
                                     out_offset=bass.IndirectOffsetOnAxis(ap=start_i[:, t:t + 1], axis=0),
                                     in_=H[:, t, :], in_offset=None,
                                     bounds_check=E - 1, oob_is_err=False).then_inc(sem(f"placed{k}"), 16)
            e.indirect_dma_start(out=lane_init[:, :], out_offset=None, in_=table[:, :],
                                 in_offset=bass.IndirectOffsetOnAxis(ap=first_i[:, 0:1], axis=0))\
                .then_inc(sem(f"lane_read{k}"), 16)

        def lane_start_sync(e, k):
            e.wait_ge(sem(f"placed{k}"), 16 * TILES)
            e.wait_ge(sem(f"lane_read{k}"), 16)
            e.dma_start(lrows(first_rows)[:, 0, :], lane_init[:, :]).then_inc(sem(f"lane_placed{k}"), 16)
            e.wait_ge(sem(f"lane_placed{k}"), 16)

        def load_fill(e, l, i, r):
            wait(e, f"filled{l}", i * R + (r - R + 2))
            gate(e)
            e.dma_start(fill[:, r, :, :], lrows(first_rows)[:, bass.ds((i * R + r) * K, K), :])\
                .then_inc(sem(f"first{l}_{r}"), 16)

        MAXQ = [list(range(a, min(a + 8, K))) for a in range(0, K, 8)]
        NQ = len(MAXQ)
        assert NQ % 2 == 0

        def pairs(cols):
            return [cols[a:a + 2] for a in range(0, len(cols), 2)]

        LASTQ = [list(range(a, min(a + 4, K))) for a in range(0, K, 4)]
        NL = len(LASTQ)

        def back(q):
            return next(m for m in range(1, NL + 1) if (q - m if q >= m else q - m + NL) % 2 == q % 2)

        GROUPS = R * K // ACC_PER_SET
        SET_GROUPS = [len(range(s, GROUPS, ACC_SETS)) for s in range(ACC_SETS)]

        def wait_slot_added(e, i, r):
            if not (isinstance(i, int) and i == 0):
                for s in range(ACC_SETS):
                    upto = len(range(s, (r + 1) * K // ACC_PER_SET, ACC_SETS))
                    wait(e, f"added{s}", i * (16 * ACC_PER_SET * SET_GROUPS[s])
                         - 16 * ACC_PER_SET * (SET_GROUPS[s] - upto))

        def acc_buf(k):
            if k == 0:
                return M
            t = ring if k % 2 else fill
            return t[:, :, :, :].rearrange("p r k f -> p (r k) f")[:, 0:TILES, :]

        block = ctx.enter_context(nc.Block())

        @block.sync
        def _(e):
            e.wait_ge(sem("x_padded"), 1)
            e.dma_start(X[0:P - 1, :, :], x[0:(P - 1) * TILES, :].rearrange("(p t) f -> p t f", t=TILES))\
                .then_inc(sem("x_in"), 16)
            e.dma_start(X[P - 1:P, 0:LAST_ROWS, :], x[(P - 1) * TILES:N, :].rearrange("(p t) f -> p t f", p=1))\
                .then_inc(sem("x_in"), 16)
            for tile, w in ((w_ab[:, 0:D], l0_w1[0:D, :]), (w_ab[:, D:2 * D], l0_w1[D:2 * D, :]),
                            (w_gcn[:, :], l1_w[:, :]), (w_hop1[:, :], l2_w1[:, :]), (w_hop2[:, :], l2_w2[:, :]),
                            (w_lastT[:, 0:D], l3_ws[:, :]), (w_lastT[:, D:2 * D], l3_wn[:, :]),
                            *((bias[n][:, :], brow(b)) for n, b in (
                                ("e1", l0_b1), ("e2", l0_b2), ("gcn", l1_b), ("hop1", l2_b1), ("hop2", l2_b2),
                                ("last", l3_bs), ("last2", l3_bn)))):
                e.dma_start(tile, w).then_inc(sem("w_in"), 16)
            e.wait_ge(sem("diag_clear"), 1)
            e.dma_start(w_diag[0:D, 0:D], l0_w2[:, :]).then_inc(sem("w_in"), 16)
            e.dma_start(w_diag[D:P, D:P], l0_w2[:, :]).then_inc(sem("w_in"), 16)
            e.dma_start(keep[:, :].bitcast(i32), dst_l).then_inc(sem("dst_in"), 16)
            e.wait_ge(sem("const"), 1)
            e.dma_start(prev_i[1:P, :], dst_l[0:P - 1, LANE - 1:LANE], allow_slow_non_contiguous=True)\
                .then_inc(sem("dst_in"), 16)
            e.wait_ge(sem("fill_clear"), 1)
            zero = fill[:, :, :, :].rearrange("p r k f -> p (r k) f")
            for c in range(0, LANE, R * K):
                e.dma_start(lrows(first_rows)[:, c:c + R * K, :], zero).then_inc(sem("zeroed"), 16)
            e.wait_ge(sem("ab_made"), 1)
            e.dma_start(nrows(tab_edge_b), M).then_inc(sem("tab0"), 16)
            e.dma_start(nrows(tab_edge_a), H).then_inc(sem("tab0"), 16)
            for r in range(R):
                pass_index(e, 0, 0, r)
            for a in accs:
                e.dma_start(a.rearrange("(p t) f -> p t f", p=P), zero[:, 0:TILES + 1, :])\
                    .then_inc(sem("acc_zeroed"), 16)
            lane_start_sync(e, 0)
            e.wait_ge(sem("acc_zeroed"), 16 * len(accs))
            for r in range(R):
                load_fill(e, 0, 0, r)
            with e.Fori(1, ITERS) as i:
                for r in range(R):
                    pass_index(e, 0, i, r)
                    load_fill(e, 0, i, r)
            for l, table in ((1, tab_gcn), (2, tab_hop1), (3, tab_hop2)):
                e.wait_ge(sem("table_made"), l)
                e.dma_start(nrows(table), H).then_inc(sem(f"tab{l}"), 16)

                def body(i):
                    for r in range(R):
                        pass_index(e, l, i, r)
                loop(e, body)
            e.wait_ge(sem("table_made"), 4)
            e.dma_start(nrows(tab_last), H).then_inc(sem("tab4"), 16)
            lane_start_sync(e, 1)

            def body4(i):
                for r in range(R):
                    wait(e, "messages", (i * R + (r - R + 1)) * NL)
                    gate(e)
                    load_fill(e, 4, i, r)
                    e.dma_start(idx[:, r, :], src_l[:, bass.ds((i * R + r) * K, K)]).then_inc(sem(f"first4_{r}"), 16)
                    e.dma_start(wblk[:, r, :], w_l[:, bass.ds((i * R + r) * K, K)]).then_inc(sem(f"first4_{r}"), 16)
            loop(e, body4)
            for s in range(ACC_SETS):
                e.wait_ge(sem(f"added{s}"), 16 * ACC_PER_SET * SET_GROUPS[s] * ITERS)
            for k, a in enumerate(accs):
                wait(e, "acc_summed", k - 2)
                e.dma_start(acc_buf(k), nrows(a[0:ROWS, :])).then_inc(sem(f"acc_in{k}"), 16)
            e.wait_ge(sem("x_final"), 1)
            e.dma_start(out[0:(P - 1) * TILES, :].rearrange("(p t) f -> p t f", t=TILES), X[0:P - 1, :, :])\
                .then_inc(sem("x_out"), 16)
            e.dma_start(out[(P - 1) * TILES:N, :].rearrange("(p t) f -> p t f", p=1), X[P - 1:P, 0:LAST_ROWS, :])\
                .then_inc(sem("x_out"), 16)
            e.wait_ge(sem("x_out"), 32)

        @block.gpsimd
        def _(e):
            chain = Chain(e, "g_chain")
            chain(e.memset(ident[:, :], 0.0))
            chain(e.memset(before[:, :], 1.0))
            chain(e.memset(earlier[:, :], 1.0))
            chain(e.affine_select(out=ident[:, :], in_=ident[:, :], compare_op=ALU.not_equal, fill=1.0,
                                  base=0, pattern=[[-1, P]], channel_multiplier=1))
            chain(e.affine_select(out=before[:, :], in_=before[:, :], compare_op=ALU.is_gt, fill=0.0,
                                  base=0, pattern=[[1, P]], channel_multiplier=-1))
            chain(e.affine_select(out=earlier[:, :], in_=earlier[:, :], compare_op=ALU.is_gt, fill=0.0,
                                  base=0, pattern=[[-1, P]], channel_multiplier=1))
            chain(e.iota(iota_i[:, :], pattern=[[1, P]], base=0, channel_multiplier=0))
            chain(e.iota(colp_i[:, 0:1], pattern=[[0, 1]], base=0, channel_multiplier=LANE))
            chain(e.iota(colp_i[:, 1:2], pattern=[[0, 1]], base=ROWS, channel_multiplier=1))
            chain(e.memset(prev_i[:, :], -1))
            e.sem_inc(sem("const"), 1)
            e.wait_ge(sem("tab0"), 32)
            for r in range(R - 1):
                gather_slot(e, 0, 0, r, tab_edge_b)
            e.wait_ge(sem("placeable"), 1)
            e.wait_ge(sem("zeroed"), 16 * (LANE // (R * K)))
            first_rows_gpsimd(e, 0, tab_edge_a)
            gather_slot(e, 0, 0, R - 1, tab_edge_b)
            with e.Fori(1, ITERS) as i:
                for r in range(R):
                    gather_slot(e, 0, i, r, tab_edge_b)
            fix_gpsimd(e, 0)
            for l, table in ((1, tab_gcn), (2, tab_hop1), (3, tab_hop2)):
                e.wait_ge(sem(f"tab{l}"), 16)

                def body(i):
                    for r in range(R):
                        gather_slot(e, l, i, r, table)
                loop(e, body)
                fix_gpsimd(e, l)
            e.wait_ge(sem("tab4"), 16)
            first_rows_gpsimd(e, 1, tab_last)
            e.wait_ge(sem("acc_zeroed"), 16 * len(accs))

            def body4(i):
                for r in range(R):
                    wait(e, "messages", (i * R + r) * NL + NL)
                    wait(e, "targets", i * R + (r + 1))
                    gate(e)
                    for g in range(K // ACC_PER_SET):
                        G = r * (K // ACC_PER_SET) + g
                        s = G % ACC_SETS
                        n = i * SET_GROUPS[s] + G // ACC_SETS
                        if not (isinstance(n, int) and n == 0):
                            wait(e, f"added{s}", n * (16 * ACC_PER_SET))
                            gate(e)
                        for a in range(ACC_PER_SET):
                            j = g * ACC_PER_SET + a
                            e.indirect_dma_start(
                                out=accs[s * ACC_PER_SET + a][:, :],
                                out_offset=bass.IndirectOffsetOnAxis(ap=idx2[:, r, j:j + 1], axis=0),
                                in_=ring[:, r, j, :], in_offset=None, compute_op=ALU.add)\
                                .then_inc(sem(f"added{s}"), 16)
            loop(e, body4)

        @block.vector
        def _(e):
            chain = Chain(e, "v_chain")
            e.memset(X[96:P, :, :], 0.0).then_inc(sem("x_padded"), 1)
            e.memset(w_diag[:, :], 0.0).then_inc(sem("diag_clear"), 1)
            e.memset(fill[:, :, :, :], 0.0).then_inc(sem("fill_clear"), 1)
            chain(e.memset(ring[:, R - 1, K - 1, :], 0.0))
            e.wait_ge(sem("const"), 1)
            chain(e.tensor_copy(iota_b[:, :], iota_i[:, :]))
            chain(e.tensor_copy(lane0[:, :], colp_i[:, 0:1]))
            chain(e.tensor_copy(spare[:, :], colp_i[:, 1:2]))
            chain(e.memset(ones[:, :], 1.0))
            chain(e.memset(carryT[:, :], 0.0))
            chain(e.memset(eps[:, :], 1e-5))
            e.wait_ge(sem("x_in"), 32)
            norm_vector(e, chain, 0)
            e.wait_ge(sem("w_in"), 16 * 16)
            chain(e.tensor_tensor(w_ab[:, 0:D], w_ab[:, 0:D], w_ab[:, D:2 * D], ALU.subtract))
            chain(e.tensor_tensor(bias["last"][:, :], bias["last"][:, :], bias["last2"][:, :], ALU.add))
            e.sem_inc(sem("normed"), 1)

            def take_ab(p, t, n):
                e.tensor_tensor(H[:, t:t + n, :], p[:, :, 0:D], brow3(bias["e1"][:, :], n), ALU.add)
                return e.tensor_copy(M[:, t:t + n, :], p[:, :, D:2 * D])
            mm_vector(e, chain, "ab", 2 * D, take_ab)
            e.sem_inc(sem("ab_made"), 1)

            e.wait_ge(sem("dst_in"), 32)
            chain(e.tensor_copy(first_i[:, :], keep[:, 0:1].bitcast(i32)))
            chain(e.tensor_copy(dst_f[:, :], keep[:, :].bitcast(i32)))
            chain(e.tensor_copy(col["first"][:, :], first_i[:, :]))
            chain(e.tensor_copy(col["prev"][:, :], prev_i[:, :]))
            chain(e.tensor_tensor(keep[:, 1:LANE], dst_f[:, 1:LANE], dst_f[:, 0:LANE - 1], ALU.is_equal))
            chain(e.memset(keep[:, 0:1], 0.0))
            loop_chain = Chain(e, "v_loop")

            def count(i):
                divide(e, loop_chain, dst_f[:, bass.ds(i * HCOLS, HCOLS)], HCOLS)
                onehots(e, "hd", i * HGRP, HGRP)
                wait(e, "hd_made", i * HGRP + HGRP)
                gate(e)
                loop_chain.clear()
            count(0)
            with e.Fori(1, HITERS) as i:
                count(i)
            e.wait_ge(sem("hd_used"), LANE // HG)
            chain(e.tensor_scalar(oh_q[:, :, :, :].rearrange("p a b c -> p (a b c)")[:, 0:LANE], dst_f[:, :], col["first"][:, 0:1], 0.0, ALU.is_equal, ALU.add,
                                  accum_out=col["cnt"][:, :]))
            chain(e.tensor_scalar(limit[:, :], keep[:, :], 2.0, -1.0, ALU.mult, ALU.add))
            chain(e.tensor_scalar(limit[:, :], limit[:, :], FULL, None, ALU.mult))
            chain(e.scalar_tensor_tensor(out=fix_i[:, :], in0=col["cnt"][:, :], scalar=-1.0, in1=lane0[:, :],
                                         op0=ALU.add, op1=ALU.add))
            chain(e.tensor_tensor(col["cont"][:, :], col["first"][:, :], col["prev"][:, :], ALU.is_equal))
            chain(e.tensor_scalar(col["whole"][:, :], col["cnt"][:, :], float(LANE), None, ALU.is_equal))
            chain(e.tensor_tensor(col["k"][:, :], col["whole"][:, :], col["cont"][:, :], ALU.mult))
            chain(e.tensor_scalar(col["contL"][:, :], col["cont"][:, :], 2.0, -1.0, ALU.mult, ALU.add))
            chain(e.tensor_scalar(col["contL"][:, :], col["contL"][:, :], FULL, None, ALU.mult))
            chain(e.tensor_copy(stat["deg"][:, :], hist[:, :]))
            chain(e.tensor_scalar(stat["has"][:, :], stat["deg"][:, :], 0.0, None, ALU.is_gt))
            chain(e.tensor_tensor_scan(out=stat["incl"][:, :], data0=ones[:, :], data1=stat["deg"][:, :],
                                       initial=0.0, op0=ALU.mult, op1=ALU.add))
            chain(e.tensor_copy(col["tot"][:, :], stat["incl"][:, TILES - 1:TILES]))
            e.sem_inc(sem("counted"), 1)
            e.wait_ge(sem("offset"), 1)
            chain(e.tensor_copy(col["offs"][:, :], pa[:, 0:1]))
            chain(e.tensor_copy(krow[:, :], pb[0:D, :]))
            chain(e.tensor_scalar(krowL[:, :], krow[:, :], 2.0, -1.0, ALU.mult, ALU.add))
            chain(e.tensor_scalar(krowL[:, :], krowL[:, :], FULL, None, ALU.mult))
            chain(e.tensor_scalar(stat["incl"][:, :], stat["incl"][:, :], col["offs"][:, 0:1], None, ALU.add))
            chain(e.tensor_scalar(stat["tmp"][:, :], stat["has"][:, :], -BEYOND, BEYOND, ALU.mult, ALU.add))
            chain(e.tensor_tensor(stat["incl"][:, :], stat["incl"][:, :], stat["tmp"][:, :], ALU.add))
            chain(e.tensor_tensor(start_i[:, :], stat["incl"][:, :], stat["deg"][:, :], ALU.subtract))
            chain(e.tensor_scalar(end_i[:, :], stat["incl"][:, :], -1.0, None, ALU.add))
            e.sem_inc(sem("placeable"), 1)
            chain(e.tensor_scalar(stat["deg"][:, :], stat["deg"][:, :], 1.0, None, ALU.max))
            chain(e.reciprocal(stat["inv"][:, :], stat["deg"][:, :]))
            e.sem_inc(sem("degrees"), 1)

            def body0(i):
                for r in range(R):
                    b = i * R + r
                    load_masks(e, loop_chain, i, r)
                    loop_chain(e.tensor_copy(mblk[:, 1, :], limit[:, bass.ds(b * K, K)]))
                    wait(e, f"first0_{r}", i * 16 + 16)
                    scan_columns(e, loop_chain, fill, r, mblk[:, 0, :], ALU.mult, ALU.add, range(K))
                    e.sem_inc(sem("filled0"), 1)
                    wait(e, f"gathered0_{r}", i * (16 * K) + 16 * K)
                    loop_chain(e.tensor_tensor(ring[:, r, :, :], ring[:, r, :, :], fill[:, r, :, :], ALU.add))
                    e.sem_inc(sem("summed0"), 1)
                    loop_chain(e.tensor_copy(srcf[:, :], idx[:, r, :]))
                    divide(e, loop_chain, srcf[:, :], K)
                    onehots(e, "hs", b * (K // HG), K // HG)
                    for q, cols in enumerate(MAXQ):
                        wait(e, "products0", b * NQ + (q + 1))
                        scan_columns(e, loop_chain, ring, r, mblk[:, 1, :], ALU.min, ALU.max, cols, om[q % 2])
                        e.sem_inc(sem("taken0"), 1)
                    loop_chain.clear()
                    e.sem_inc(sem("scanned"), 1)
            loop(e, body0)
            fix_vector(e, chain, 0, ALU.min, ALU.max, krowL, col["contL"])
            e.wait_ge(sem("hs_used"), LANE // HG)
            chain(e.tensor_scalar(stat["nsrc"][:, :], hist[:, :], 1.0, None, ALU.max))
            e.sem_inc(sem("degrees"), 1)
            e.wait_ge(sem("rooted"), 2)
            chain(e.reciprocal(stat["nsrc"][:, :], stat["nsrc"][:, :]))
            chain(e.reciprocal(stat["ndst"][:, :], stat["ndst"][:, :]))
            e.wait_ge(sem("node_rows0"), 16 * TILES)
            chain(e.tensor_tensor(M, M, brow3(bias["e2"][:, :], TILES), ALU.add))
            chain(e.tensor_tensor(H, M, M, ALU.subtract))
            chain(e.scalar_tensor_tensor(out=H.bitcast(i32), in0=H, scalar=0.0, in1=bcast(stat["has"][:, :]),
                                         op0=ALU.is_equal, op1=ALU.mult))
            chain(e.tensor_tensor(M, M, X[:, :, :], ALU.add))
            chain(e.copy_predicated(X[:, :, :], H.bitcast(i32), M))

            norm_vector(e, chain, 1)
            chain(e.tensor_tensor(H, H, bcast(stat["nsrc"][:, :]), ALU.mult))
            e.sem_inc(sem("table_made"), 1)
            sum_pass_vector(e, 1)
            fix_vector(e, chain, 1, ALU.mult, ALU.add, krow, col["cont"])
            e.wait_ge(sem("node_rows1"), 16 * TILES)
            chain(e.tensor_tensor(M, M, bcast(stat["ndst"][:, :]), ALU.mult))
            e.sem_inc(sem("aggregated"), 1)

            def take_gcn(p, t, n):
                h, xs = H[:, t:t + n, :], X[:, t:t + n, :]
                chain(e.tensor_tensor(h, p, brow3(bias["gcn"][:, :], n), ALU.add))
                chain(e.scalar_tensor_tensor(out=h, in0=h, scalar=0.01, in1=h, op0=ALU.mult, op1=ALU.max))
                return e.tensor_tensor(xs, xs, h, ALU.add)
            mm_vector(e, chain, "gcn", D, take_gcn)

            norm_vector(e, chain, 2)
            e.sem_inc(sem("table_made"), 1)
            sum_pass_vector(e, 2)
            fix_vector(e, chain, 2, ALU.mult, ALU.add, krow, col["cont"])
            e.wait_ge(sem("node_rows2"), 16 * TILES)
            chain(e.tensor_tensor(M, M, bcast(stat["inv"][:, :]), ALU.mult))
            e.sem_inc(sem("aggregated"), 1)

            def take_hop1(p, t, n):
                h = H[:, t:t + n, :]
                chain(e.tensor_tensor(h, p, brow3(bias["hop1"][:, :], n), ALU.add))
                return e.tensor_scalar(h, h, 0.0, None, ALU.max)
            mm_vector(e, chain, "hop1", D, take_hop1)
            e.sem_inc(sem("table_made"), 1)

            sum_pass_vector(e, 3)
            fix_vector(e, chain, 3, ALU.mult, ALU.add, krow, col["cont"])
            e.wait_ge(sem("node_rows3"), 16 * TILES)
            chain(e.tensor_tensor(M, M, bcast(stat["inv"][:, :]), ALU.mult))
            e.sem_inc(sem("aggregated"), 1)

            def take_add(name):
                def take(p, t, n):
                    h, xs = H[:, t:t + n, :], X[:, t:t + n, :]
                    chain(e.tensor_tensor(h, p, brow3(bias[name][:, :], n), ALU.add))
                    return e.tensor_tensor(xs, xs, h, ALU.add)
                return take
            mm_vector(e, chain, "hop2", D, take_add("hop2"))

            e.wait_ge(sem("w_turned"), 1)
            chain(e.tensor_copy(w_last[:, :], pa[:, 0:D]))
            e.sem_inc(sem("w_copied"), 1)
            norm_vector(e, chain, 3)
            e.sem_inc(sem("table_made"), 1)

            def body4(i):
                for r in range(R):
                    b = i * R + r
                    load_masks(e, loop_chain, i, r)
                    wait(e, f"first4_{r}", i * 48 + 48)
                    loop_chain(e.tensor_copy(srcf[:, :], idx[:, r, :]))
                    e.sem_inc(sem("numbered"), 1)
                    scan_columns(e, loop_chain, fill, r, mblk[:, 0, :], ALU.mult, ALU.add, range(K))
                    e.sem_inc(sem("filled4"), 1)
                    for q, cols in enumerate(LASTQ):
                        g = b * NL + q
                        wait(e, "spread", g + 1)
                        wait(e, "products4", b * NL + (q + 1 - back(q)))
                        wait(e, "matched", b * NL + (q + 1 - back(q)))
                        for k, j in enumerate(cols):
                            row = tp[q % 2][:, k * P:(k + 1) * P]
                            e.tensor_scalar(eqw[:, q % 2, k, :], row, srcf[:, j:j + 1], wblk[:, r, j:j + 1],
                                            ALU.is_equal, ALU.mult)
                            last = e.scalar_tensor_tensor(out=dupjunk[:, q % 2, k, :], in0=row, scalar=srcf[:, j:j + 1],
                                                          in1=earlier[:, :], op0=ALU.is_equal, op1=ALU.mult,
                                                          accum_out=dupc[:, j:j + 1])
                        last.then_inc(sem("matched"), 1)
                    wait(e, "matched", b * NL + NL)
                    loop_chain(e.tensor_scalar(dup1[:, :], dupc[:, :], 0.0, None, ALU.is_gt))
                    loop_chain(e.tensor_scalar(dup2[:, :], srcf[:, :], -1.0, spare[:, 0:1], ALU.mult, ALU.add))
                    loop_chain(e.tensor_tensor(dup2[:, :], dup2[:, :], dup1[:, :], ALU.mult))
                    wait_slot_added(e, i, r)
                    loop_chain(e.tensor_tensor(idx2[:, r, :], dup2[:, :], srcf[:, :], ALU.add))
                    loop_chain.clear()
                    e.sem_inc(sem("targets"), 1)
            loop(e, body4)
            e.wait_ge(sem("acc_in0"), 16)
            for k in range(1, len(accs)):
                e.wait_ge(sem(f"acc_in{k}"), 16)
                chain(e.tensor_tensor(M, M, acc_buf(k), ALU.add))
                e.sem_inc(sem("acc_summed"), 1)
            e.sem_inc(sem("aggregated"), 1)
            mm_vector(e, chain, "last", D, take_add("last"))
            e.sem_inc(sem("x_final"), 1)

        @block.scalar
        def _(e):
            norm_scalar(e, 0)
            mm_scalar(e, "ab", D)
            e.wait_ge(sem("degrees"), 1)
            e.activation(stat["ndst"][:, :], stat["deg"][:, :], ACT.Sqrt).then_inc(sem("rooted"), 1)

            def body0(i):
                for r in range(R):
                    b = i * R + r
                    wait(e, "summed0", b + 1)
                    e.activation(ring[:, r, :, :], ring[:, r, :, :], ACT.Relu).then_inc(sem("relued0"), 1)
                    for q, cols in enumerate(MAXQ):
                        rows, w = (P, len(cols) // 2 * P) if len(cols) > 1 else (D, P)
                        wait(e, "turned0", b * NQ + (q + 1))
                        wait(e, "products0", b * NQ + (q - 1))
                        e.activation(hT[0:rows, q % 2, 0:w], tp[q % 2][0:rows, 0:w], ACT.Copy)\
                            .then_inc(sem("copied0"), 1)
                    pass_store(e, 0, i, r)
            loop(e, body0)
            e.wait_ge(sem("degrees"), 2)
            e.activation(stat["nsrc"][:, :], stat["nsrc"][:, :], ACT.Sqrt).then_inc(sem("rooted"), 1)
            for l, name, kd in ((1, "gcn", D), (2, "hop1", 2 * D), (3, "hop2", 2 * D)):
                if l < 3:
                    norm_scalar(e, l)

                def body(i):
                    for r in range(R):
                        pass_store(e, l, i, r)
                loop(e, body)
                mm_scalar(e, name, kd)
            norm_scalar(e, 3)

            def body4(i):
                for r in range(R):
                    b = i * R + r
                    wait_slot_added(e, i, r)
                    for q, cols in enumerate(LASTQ):
                        wait(e, "products4", b * NL + (q + 1))
                        e.activation(ring[:, r, cols[0]:cols[-1] + 1, :],
                                     om[q % 2][:, 0:len(cols) * D].rearrange("p (k f) -> p k f", f=D), ACT.Copy)\
                            .then_inc(sem("messages"), 1)
            loop(e, body4)
            mm_scalar(e, "last", 2 * D)

        @block.tensor
        def _(e):
            e.wait_ge(sem("const"), 1)
            e.wait_ge(sem("normed"), 1)
            mm_tensor(e, "ab", 0, D, w_ab[:, :], 2 * D)
            count_tensor(e, "hd", 0, HGRP, True)
            with e.Fori(1, HITERS) as i:
                count_tensor(e, "hd", i * HGRP, HGRP, False)
            e.wait_ge(sem("counted"), 1)
            e.matmul(pa[:, 0:1], before[:, :], col["tot"][:, :], start=True, stop=True)
            e.matmul(pb[0:D, :], col["k"][:, 0:1].broadcast_to([P, D]), ident[:, :], start=True, stop=True)\
                .then_inc(sem("offset"), 1)
            e.wait_ge(sem("placeable"), 1)

            def body0(i):
                for r in range(R):
                    b = i * R + r
                    wait(e, "relued0", b + 1)
                    for q, cols in enumerate(MAXQ):
                        wait(e, "copied0", b * NQ + (q - 1))
                        gate(e)
                        for k, c in enumerate(pairs(cols)):
                            m = len(c) * D
                            last = e.transpose(tp[q % 2][0:m, k * P:(k + 1) * P],
                                               ring[:, r, c[0]:c[-1] + 1, :], ident[:, :])
                        last.then_inc(sem("turned0"), 1)
                        wait(e, "copied0", b * NQ + (q + 1))
                        wait(e, "taken0", b * NQ + (q - 1))
                        for k, c in enumerate(pairs(cols)):
                            m = len(c) * D
                            last = e.matmul(om[q % 2][:, k * P:k * P + m], hT[0:m, q % 2, k * P:(k + 1) * P],
                                            w_diag[0:m, 0:m], start=True, stop=True)
                        last.then_inc(sem("products0"), 1)
                    count_tensor(e, "hs", b * (K // HG), K // HG, isinstance(i, int) and r == 0)
            loop(e, body0)
            fix_tensor(e, 0)
            for l, name, c0, rhs in ((1, "gcn", D, w_gcn), (2, "hop1", 0, w_hop1), (3, "hop2", 0, w_hop2)):
                fix_tensor(e, l)
                e.wait_ge(sem("aggregated"), l)
                mm_tensor(e, name, c0, 2 * D, rhs[:, :], D)
            e.transpose(pa[:, 0:D], w_lastT[:, :], ident[0:D, 0:D]).then_inc(sem("w_turned"), 1)

            def spread(b, q, cols):
                wait(e, "matched", b * NL + (q + 1 - back(q)))
                for k, j in enumerate(cols):
                    last = e.matmul(tp[q % 2][:, k * P:(k + 1) * P], srcf[:, j:j + 1].broadcast_to([P, P]),
                                    ident[:, :], start=True, stop=True)
                last.then_inc(sem("spread"), 1)

            def body4(i):
                for r in range(R):
                    b = i * R + r
                    wait(e, "numbered", b + 1)
                    spread(b, 0, LASTQ[0])
                    for q, cols in enumerate(LASTQ):
                        if q + 1 < NL:
                            spread(b, q + 1, LASTQ[q + 1])
                        if q == 0:
                            wait(e, "filled4", b + 1)
                        wait(e, "matched", b * NL + (q + 1))
                        wait(e, "messages", b * NL + (q + 1 - back(q)))
                        for k, j in enumerate(cols):
                            last = e.matmul(om[q % 2][:, k * D:(k + 1) * D], eqw[:, q % 2, k, :],
                                            fill[:, r, j, :], start=True, stop=True)
                        last.then_inc(sem("products4"), 1)
            loop(e, body4)
            e.wait_ge(sem("w_copied"), 1)
            e.wait_ge(sem("aggregated"), 4)
            mm_tensor(e, "last", 0, 2 * D, w_last[:, :], D)


_INS = ["x", "src", "dst", "edge_weight", "L0_gnn_W1", "L0_gnn_b1", "L0_gnn_W2", "L0_gnn_b2", "L1_gnn_W",
        "L1_gnn_b", "L2_gnn_W1", "L2_gnn_b1", "L2_gnn_W2", "L2_gnn_b2", "L3_gnn_W_self", "L3_gnn_b_self",
        "L3_gnn_W_neigh", "L3_gnn_b_neigh"]


def kernel(**inputs):
    import numpy as _np
    import concourse.bacc as _bacc
    from concourse import mybir as _mybir
    from concourse.bass_utils import run_bass_kernel_spmd as _run

    nc = _bacc.Bacc("TRN2", target_bir_lowering=False, num_devices=1)
    arrays, args = {}, []
    for name in _INS:
        a = _np.ascontiguousarray(inputs[name])
        arrays["in_" + name] = a
        args.append(nc.dram_tensor("in_" + name, a.shape, _mybir.dt.from_np(a.dtype), kind="ExternalInput").ap())
    args.append(nc.dram_tensor("out_0", (N, D), _mybir.dt.float32, kind="ExternalOutput").ap())
    build(nc, *args)
    return _run(nc, [arrays], core_ids=[0]).results[0]["out_0"]
```

```python
import concourse.bass as bass
from concourse import mybir
from contextlib import ExitStack

N, E, D = 12500, 400000, 64
P = 128
TILES = -(-N // P)
ROWS = P * TILES
LANE = E // P
K = 25
R = 5
BLOCKS = LANE // K
ITERS = BLOCKS // R
HG = 5
HBUF = 5
CHUNK = 25
PIVOTS = LANE // CHUNK
NT = 7
NGROUPS = TILES // NT
ACC_SETS, ACC_PER_SET = 2, 5
FULL = 3.4028234663852886e38
LAST_ROWS = N - (P - 1) * TILES
BEYOND = 2.0 * E


def build(nc, x, src, dst, edge_weight, l0_w1, l0_b1, l0_w2, l0_b2, l1_w, l1_b,
          l2_w1, l2_b1, l2_w2, l2_b2, l3_ws, l3_bs, l3_wn, l3_bn, out):
    f32, bf16, i32 = mybir.dt.float32, mybir.dt.bfloat16, mybir.dt.int32
    ALU, ACT, AX = mybir.AluOpType, mybir.ActivationFunctionType, mybir.AxisListType
    assert N <= ROWS and E == P * LANE and LANE == K * R * ITERS and BLOCKS == R * ITERS
    ctx = ExitStack()
    with ctx:
        def sb(name, shape, dt=f32):
            return ctx.enter_context(nc.sbuf_tensor(name, shape, dt))

        def ps(name, shape):
            return ctx.enter_context(nc.psum_tensor(name, shape, f32))

        sems = {}

        def sem(name):
            if name not in sems:
                sems[name] = ctx.enter_context(nc.semaphore(name))
            return sems[name]

        def dram(name, shape, dt=f32):
            return nc.dram_tensor(name, shape, dt).ap()

        tab_edge_a = dram("tab_edge_a", (ROWS, D))
        tab_edge_b = dram("tab_edge_b", (ROWS, D))
        tab_gcn = dram("tab_gcn", (ROWS, D))
        tab_hop1 = dram("tab_hop1", (ROWS, D))
        tab_hop2 = dram("tab_hop2", (ROWS, D))
        tab_last = dram("tab_last", (ROWS, D))
        edge_rows = dram("edge_rows", (E, D))
        first_rows = dram("first_rows", (E, D))
        accs = [dram(f"acc{k}", (ROWS + P, D)) for k in range(ACC_SETS * ACC_PER_SET)]

        X = sb("X", [P, TILES, D])
        HM = sb("HM", [P, TILES, 2 * D])
        H, M = HM[:, :, 0:D], HM[:, :, D:2 * D]
        dst_f = sb("dst_f", [P, LANE])
        limit = dst_f
        keep = sb("keep", [P, LANE])
        ring = sb("ring", [P, R, K, D])
        fill = sb("fill", [P, R, K, D])
        idx = sb("idx", [P, R, K], i32)
        idx2 = sb("idx2", [P, R, K], i32)
        wblk = sb("wblk", [P, R, K])
        mblk = sb("mblk", [P, 2, K])
        srcf = sb("srcf", [P, K])
        dupc = sb("dupc", [P, K])
        dup1 = sb("dup1", [P, K])
        dup2 = sb("dup2", [P, K])
        dupjunk = sb("dupjunk", [P, 2, 4, P], bf16)
        hT = sb("hT", [P, 2, 512])
        eqw = sb("eqw", [P, 2, 4, P])
        oh_q = sb("oh_q", [P, HBUF, HG, P], bf16)
        oh_r = sb("oh_r", [P, HBUF, HG, TILES], bf16)
        hq, hr, ht = (sb(n, [P, PIVOTS]) for n in ("hq", "hr", "ht"))
        hi = sb("hi", [P, PIVOTS], i32)
        pivot = sb("pivot", [P, PIVOTS])
        ident = sb("ident", [P, P])
        before = sb("before", [P, P])
        earlier = sb("earlier", [P, P])
        iota_i = sb("iota_i", [P, P], i32)
        iota_b = sb("iota_b", [P, P], bf16)
        colp_i = sb("colp_i", [P, 2], i32)
        lane0 = sb("lane0", [P, 1])
        spare = sb("spare", [P, 1])
        ones = sb("ones", [P, TILES])
        w_ab = sb("w_ab", [D, 2 * D])
        w_diag = sb("w_diag", [P, P])
        w_gcn = sb("w_gcn", [D, D])
        w_hop1 = sb("w_hop1", [P, D])
        w_hop2 = sb("w_hop2", [P, D])
        node_f = sb("node_f", [P, TILES + 1])
        node_i = sb("node_i", [P, TILES + 1], i32)
        chunk_f = sb("chunk_f", [P, TILES + 1])
        chunk_i = sb("chunk_i", [P, TILES + 1], i32)
        edge0 = sb("edge0", [P, TILES + 1])
        w_lastT = sb("w_lastT", [D, 2 * D])
        w_last = sb("w_last", [P, D])
        bias = {n: sb("bias_" + n, [P, D]) for n in ("e1", "e2", "gcn", "hop1", "hop2", "last", "last2")}
        stat = {n: sb("stat_" + n, [P, TILES]) for n in
                ("mean", "var", "rstd", "deg", "has", "incl", "nsrc", "ndst", "inv", "tmp")}
        eps = sb("eps", [P, 1])
        start_i = sb("start_i", [P, TILES], i32)
        end_i = sb("end_i", [P, TILES], i32)
        fix_i = sb("fix_i", [P, 1], i32)
        first_i = sb("first_i", [P, 1], i32)
        prev_i = sb("prev_i", [P, 1], i32)
        col = {n: sb("col_" + n, [P, 1]) for n in
               ("first", "prev", "cnt", "cont", "whole", "k", "contL", "offs", "tot")}
        krow = sb("krow", [D, P])
        krowL = sb("krowL", [D, P])
        carryT = sb("carryT", [D, P + 1])
        tail = sb("tail", [P, D])
        fixrow = sb("fixrow", [P, D])
        zero_row = sb("zero_row", [P, D])
        lane_init = sb("lane_init", [P, D])

        tp = [ps(f"tp{k}", [P, 512]) for k in range(2)]
        om = [ps(f"om{k}", [P, 512]) for k in range(2)]
        hist = ps("hist", [P, TILES])
        pa = ps("pa", [P, P])
        pb = ps("pb", [P, P])

        chunks = ring[:, :, :, :].rearrange("p r k f -> p (r k) f")

        lanes = lambda a: a.rearrange("(p c) -> p c", p=P)
        lrows = lambda a: a.rearrange("(p c) f -> p c f", p=P)
        nrows = lambda a: a.rearrange("(p t) f -> p t f", p=P)
        src_l, dst_l, w_l = lanes(src), lanes(dst), lanes(edge_weight)
        flat = lambda a: a.rearrange("p a b -> p (a b)")
        brow = lambda b: b.rearrange("(a n) -> a n", a=1).partition_broadcast(P)

        def wait(e, name, n):
            if not (isinstance(n, int) and n <= 0):
                e.wait_ge(sem(name), n)

        def gate(e):
            e.sem_inc(sem("gate_" + e.engine.name), 1)

        def loop(e, body):
            body(0)
            with e.Fori(1, ITERS) as i:
                body(i)

        class Chain:
            def __init__(self, e, name):
                self.e, self.name, self.n = e, name, 0

            def __call__(self, ins):
                self.n += 1
                ins.then_inc(sem(self.name), 1)
                self.e.wait_ge(sem(self.name), self.n)

            def clear(self):
                self.e.sem_clear(sem(self.name))
                self.n = 0

        def bcast(ap2, n=D):
            return ap2.unsqueeze(2).broadcast_to([P, ap2.shape[1], n])

        def brow3(b, n):
            return b.unsqueeze(1).broadcast_to([P, n, D])

        SUB = [range(a, min(a + 4, NT)) for a in range(0, NT, 4)]
        assert len(SUB) % 2 == 0 and TILES == NT * NGROUPS
        MM = {n: k * NGROUPS * len(SUB) for k, n in enumerate(("ab", "gcn", "hop1", "hop2", "last"))}

        def batches(name, g):
            return [(MM[name] + g * len(SUB) + q, q % 2, [g * NT + t for t in ts]) for q, ts in enumerate(SUB)]

        def mm_tensor(e, name, g, c0, c1, rhs, m):
            kd = c1 - c0
            for n, u, ts in batches(name, g):
                wait(e, "mm_copied", n - 1)
                for k, t in enumerate(ts):
                    last = e.transpose(tp[u][0:kd, k * P:(k + 1) * P], HM[:, t, c0:c1], ident[:, :])
                last.then_inc(sem("mm_turned"), 1)
                wait(e, "mm_copied", n + 1)
                wait(e, "mm_taken", n - 1)
                for k, t in enumerate(ts):
                    last = e.matmul(om[u][:, k * m:(k + 1) * m], hT[0:kd, u, k * P:(k + 1) * P],
                                    rhs, start=True, stop=True)
                last.then_inc(sem("mm_done"), 1)

        def mm_scalar(e, name, g, kd):
            for n, u, ts in batches(name, g):
                wait(e, "mm_turned", n + 1)
                wait(e, "mm_done", n - 1)
                e.activation(hT[0:kd, u, 0:len(ts) * P], tp[u][0:kd, 0:len(ts) * P], ACT.Copy)\
                    .then_inc(sem("mm_copied"), 1)

        def mm_vector(e, name, g, m, take):
            for n, u, ts in batches(name, g):
                wait(e, "mm_done", n + 1)
                take(om[u][:, 0:len(ts) * m].rearrange("p (n m) -> p n m", n=len(ts)), ts[0], len(ts))\
                    .then_inc(sem("mm_taken"), 1)
            e.wait_ge(sem("mm_taken"), n + 1)

        def norm_vector(e, chain, l, g):
            ts = slice(g * NT, (g + 1) * NT)
            xs, h, m = X[:, ts, :], H[:, ts, :], M[:, ts, :]
            mean, var, rstd = (stat[n][:, ts] for n in ("mean", "var", "rstd"))
            chain(e.tensor_reduce(out=mean, in_=xs, op=ALU.add, axis=AX.X))
            chain(e.tensor_scalar(mean, mean, 1.0 / D, None, ALU.mult))
            chain(e.tensor_tensor(h, xs, bcast(mean), ALU.subtract))
            chain(e.tensor_tensor(m, h, h, ALU.mult))
            e.tensor_reduce(out=var, in_=m, op=ALU.add, axis=AX.X).then_inc(sem("var"), 1)
            e.wait_ge(sem("std"), l * NGROUPS + g + 1)
            chain(e.reciprocal(rstd, rstd))
            chain(e.scalar_tensor_tensor(out=h, in0=h, scalar=0.0, in1=bcast(rstd), op0=ALU.max, op1=ALU.mult))

        def norm_scalar(e, l, g):
            ts = slice(g * NT, (g + 1) * NT)
            e.wait_ge(sem("var"), l * NGROUPS + g + 1)
            e.activation(stat["rstd"][:, ts], stat["var"][:, ts], ACT.Sqrt, bias=eps[:, 0:1], scale=1.0 / D)\
                .then_inc(sem("std"), 1)

        def divide(e, chain, val, n):
            q, r, t, ti = hq[:, 0:n], hr[:, 0:n], ht[:, 0:n], hi[:, 0:n]
            chain(e.tensor_scalar(ti, val, 1.0 / TILES, None, ALU.mult))
            chain(e.tensor_copy(q, ti))
            chain(e.scalar_tensor_tensor(out=r, in0=q, scalar=-float(TILES), in1=val, op0=ALU.mult, op1=ALU.add))
            chain(e.tensor_scalar(t, r, 0.0, None, ALU.is_lt))
            chain(e.tensor_tensor(q, q, t, ALU.subtract))
            chain(e.scalar_tensor_tensor(out=r, in0=t, scalar=float(TILES), in1=r, op0=ALU.mult, op1=ALU.add))
            chain(e.tensor_scalar(t, r, float(TILES), None, ALU.is_ge))
            chain(e.tensor_tensor(q, q, t, ALU.add))
            chain(e.scalar_tensor_tensor(out=r, in0=t, scalar=-float(TILES), in1=r, op0=ALU.mult, op1=ALU.add))

        def onehots(e, name, base, groups):
            for g in range(groups):
                k = g % HBUF
                wait(e, name + "_used", base + g - HBUF + 1)
                for c in range(HG):
                    j = g * HG + c
                    e.tensor_scalar(oh_q[:, k, c, :], iota_b[:, :], hq[:, j:j + 1], None, ALU.is_equal)
                    last = e.tensor_scalar(oh_r[:, k, c, :], iota_b[:, 0:TILES], hr[:, j:j + 1], None, ALU.is_equal)
                last.then_inc(sem(name + "_made"), 1)

        def count_tensor(e, name, base, groups, first):
            for g in range(groups):
                k = g % HBUF
                wait(e, name + "_made", base + g + 1)
                for c in range(HG):
                    last = e.matmul(hist[:, :], oh_q[:, k, c, :], oh_r[:, k, c, :],
                                    start=first and g == 0 and c == 0, stop=c == HG - 1,
                                    skip_group_check=True)
                last.then_inc(sem(name + "_used"), 1)

        PGRP = PIVOTS // HG

        def gather_slot(e, l, i, r, table):
            wait(e, f"indexed{r}", i * 16 + (l * 16 * ITERS + 16))
            gate(e)
            for j in range(K):
                e.indirect_dma_start(out=ring[:, r, j, :], out_offset=None, in_=table[:, :],
                                     in_offset=bass.IndirectOffsetOnAxis(ap=idx[:, r, j:j + 1], axis=0))\
                    .then_inc(sem(f"gathered{l}_{r}"), 16)

        def pass_index(e, l, i, r):
            wait(e, f"gathered{l}_{r}", i * (16 * K))
            gate(e)
            wait(e, "scanned", l * BLOCKS if isinstance(i, int) else i * R + (l * BLOCKS + r - R + 2))
            gate(e)
            wait(e, f"stored{r}", i * 16 + l * 16 * ITERS)
            gate(e)
            e.dma_start(idx[:, r, :], src_l[:, bass.ds((i * R + r) * K, K)]).then_inc(sem(f"indexed{r}"), 16)

        def pass_store(e, l, i, r):
            wait(e, "scanned", i * R + (l * BLOCKS + r + 1))
            e.dma_start(lrows(edge_rows)[:, bass.ds((i * R + r) * K, K), :], ring[:, r, :, :])\
                .then_inc(sem(f"stored{r}"), 16)

        def load_masks(e, chain, i, r):
            chain(e.tensor_copy(mblk[:, 0, :], keep[:, bass.ds((i * R + r) * K, K)]))

        def scan_columns(e, chain, buf, b, r, mask, op0, op1, cols, other=None):
            for n, j in enumerate(cols):
                prev = buf[:, r, j - 1, :] if j else buf[:, (r - 1) % R, K - 1, :]
                if isinstance(b, int) and b + j == 0:
                    prev = zero_row[:, :]
                this = buf[:, r, j, :] if other is None else other[:, n * D:(n + 1) * D]
                chain(e.scalar_tensor_tensor(out=buf[:, r, j, :], in0=prev, scalar=mask[:, j:j + 1],
                                             in1=this, op0=op0, op1=op1))

        def sum_pass_vector(e, l):
            chain = Chain(e, "v_loop")
            chain(e.memset(M, 0.0))
            if l == 2:
                chain(e.memset(fill[:, :, :, :], 0.0))
                e.sem_inc(sem("fill_clear"), 1)
            chain.clear()
            e.sem_inc(sem("cleared"), 1)

            def body(i):
                for r in range(R):
                    load_masks(e, chain, i, r)
                    wait(e, f"gathered{l}_{r}", i * (16 * K) + 16 * K)
                    scan_columns(e, chain, ring, i * R + r, r, mblk[:, 0, :], ALU.mult, ALU.add, range(K))
                    chain.clear()
                    e.sem_inc(sem("scanned"), 1)
            loop(e, body)

        def fix_tensor(e, l):
            e.wait_ge(sem("tailed"), l + 1)
            e.transpose(pa[0:D, 0:P], tail[:, :], ident[:, :]).then_inc(sem("tail_turned"), 1)
            e.wait_ge(sem("carried"), l + 1)
            e.transpose(pb[:, 0:D], carryT[:, 0:P], ident[0:D, 0:D]).then_inc(sem("carry_turned"), 1)

        def fix_vector(e, chain, l, op0, op1, row, colc):
            e.tensor_copy(tail[:, :], ring[:, R - 1, K - 1, :]).then_inc(sem("tailed"), 1)
            e.wait_ge(sem("tail_turned"), l + 1)
            e.tensor_tensor_scan(out=carryT[:, 1:P + 1], data0=row[:, :], data1=pa[0:D, 0:P], initial=0.0,
                                 op0=op0, op1=op1).then_inc(sem("carried"), 1)
            e.wait_ge(sem("carry_turned"), l + 1)
            e.wait_ge(sem("fix_read"), 16 * (l + 1))
            e.scalar_tensor_tensor(out=fixrow[:, :], in0=pb[:, 0:D], scalar=colc[:, 0:1], in1=fixrow[:, :],
                                   op0=op0, op1=op1).then_inc(sem("fix_made"), 1)

        def fix_gpsimd(e, l):
            for r in range(R):
                e.wait_ge(sem(f"stored{r}"), 16 * ITERS * (l + 1))
            e.indirect_dma_start(out=fixrow[:, :], out_offset=None, in_=edge_rows[:, :],
                                 in_offset=bass.IndirectOffsetOnAxis(ap=fix_i[:, 0:1], axis=0))\
                .then_inc(sem("fix_read"), 16)
            e.wait_ge(sem("fix_made"), l + 1)
            e.indirect_dma_start(out=edge_rows[:, :], out_offset=bass.IndirectOffsetOnAxis(ap=fix_i[:, 0:1], axis=0),
                                 in_=fixrow[:, :], in_offset=None).then_inc(sem("fix_written"), 16)
            e.wait_ge(sem("fix_written"), 16 * (l + 1))
            e.wait_ge(sem("cleared"), l + 1)
            for t in range(TILES):
                e.indirect_dma_start(out=M[:, t, :], out_offset=None, in_=edge_rows[:, :],
                                     in_offset=bass.IndirectOffsetOnAxis(ap=end_i[:, t:t + 1], axis=0),
                                     bounds_check=E - 1, oob_is_err=False).then_inc(sem(f"node_rows{t // NT}"), 16)

        def first_rows_gpsimd(e, k, table):
            for t in range(TILES):
                e.indirect_dma_start(out=first_rows[:, :],
                                     out_offset=bass.IndirectOffsetOnAxis(ap=start_i[:, t:t + 1], axis=0),
                                     in_=H[:, t, :], in_offset=None,
                                     bounds_check=E - 1, oob_is_err=False).then_inc(sem(f"placed{k}"), 16)
            e.indirect_dma_start(out=lane_init[:, :], out_offset=None, in_=table[:, :],
                                 in_offset=bass.IndirectOffsetOnAxis(ap=first_i[:, 0:1], axis=0))\
                .then_inc(sem(f"lane_read{k}"), 16)

        def lane_start_sync(e, k):
            e.wait_ge(sem(f"placed{k}"), 16 * TILES)
            e.wait_ge(sem(f"lane_read{k}"), 16)
            e.dma_start(lrows(first_rows)[:, 0, :], lane_init[:, :]).then_inc(sem(f"lane_placed{k}"), 16)
            e.wait_ge(sem(f"lane_placed{k}"), 16)

        def load_fill(e, l, i, r):
            if not isinstance(i, int):
                wait(e, f"filled{l}", i * R + (r - R + 2))
                gate(e)
            e.dma_start(fill[:, r, :, :], lrows(first_rows)[:, bass.ds((i * R + r) * K, K), :])\
                .then_inc(sem(f"first{l}_{r}"), 16)

        MAXQ = [list(range(a, min(a + 8, K))) for a in range(0, K, 8)]
        NQ = len(MAXQ)
        assert NQ % 2 == 0

        def pairs(cols):
            return [cols[a:a + 2] for a in range(0, len(cols), 2)]

        LASTQ = [list(range(a, min(a + 4, K))) for a in range(0, K, 4)]
        NL = len(LASTQ)

        def back(q):
            return next(m for m in range(1, NL + 1) if (q - m if q >= m else q - m + NL) % 2 == q % 2)

        GROUPS = R * K // ACC_PER_SET
        SET_GROUPS = [len(range(s, GROUPS, ACC_SETS)) for s in range(ACC_SETS)]

        def wait_slot_added(e, i, r):
            if not (isinstance(i, int) and i == 0):
                for s in range(ACC_SETS):
                    upto = len(range(s, (r + 1) * K // ACC_PER_SET, ACC_SETS))
                    wait(e, f"added{s}", i * (16 * ACC_PER_SET * SET_GROUPS[s])
                         - 16 * ACC_PER_SET * (SET_GROUPS[s] - upto))

        def acc_buf(g, k):
            t = (ring if g % 2 else fill)[:, :, :, :].rearrange("p r k f -> p (r k) f")
            return t[:, k * NT:(k + 1) * NT, :]

        block = ctx.enter_context(nc.Block())

        def store_table(e, l, table):
            for g in range(NGROUPS):
                ts = slice(g * NT, (g + 1) * NT)
                e.wait_ge(sem("table_made"), (l - 1) * NGROUPS + g + 1)
                e.dma_start(nrows(table)[:, ts, :], H[:, ts, :]).then_inc(sem(f"tab{l}"), 16)

        @block.sync
        def _(e):
            e.dma_start(keep[:, :].bitcast(i32), dst_l).then_inc(sem("dst_in"), 16)
            e.wait_ge(sem("const"), 1)
            e.dma_start(prev_i[1:P, :], dst_l[0:P - 1, LANE - 1:LANE], allow_slow_non_contiguous=True)\
                .then_inc(sem("dst_in"), 16)
            e.wait_ge(sem("x_padded"), 1)
            e.dma_start(X[0:P - 1, :, :], x[0:(P - 1) * TILES, :].rearrange("(p t) f -> p t f", t=TILES))\
                .then_inc(sem("x_in"), 16)
            e.dma_start(X[P - 1:P, 0:LAST_ROWS, :], x[(P - 1) * TILES:N, :].rearrange("(p t) f -> p t f", p=1))\
                .then_inc(sem("x_in"), 16)
            for tile, w in ((w_ab[:, 0:D], l0_w1[0:D, :]), (w_ab[:, D:2 * D], l0_w1[D:2 * D, :]),
                            (w_gcn[:, :], l1_w[:, :]), (w_hop1[:, :], l2_w1[:, :]), (w_hop2[:, :], l2_w2[:, :]),
                            (w_lastT[:, 0:D], l3_ws[:, :]), (w_lastT[:, D:2 * D], l3_wn[:, :]),
                            *((bias[n][:, :], brow(b)) for n, b in (
                                ("e1", l0_b1), ("e2", l0_b2), ("gcn", l1_b), ("hop1", l2_b1), ("hop2", l2_b2),
                                ("last", l3_bs), ("last2", l3_bn)))):
                e.dma_start(tile, w).then_inc(sem("w_in"), 16)
            e.wait_ge(sem("diag_clear"), 1)
            e.dma_start(w_diag[0:D, 0:D], l0_w2[:, :]).then_inc(sem("w_in"), 16)
            e.dma_start(w_diag[D:P, D:P], l0_w2[:, :]).then_inc(sem("w_in"), 16)
            for r in range(R):
                pass_index(e, 0, 0, r)
            for g in range(NGROUPS):
                ts = slice(g * NT, (g + 1) * NT)
                e.wait_ge(sem("ab_made"), g + 1)
                e.dma_start(nrows(tab_edge_b)[:, ts, :], M[:, ts, :]).then_inc(sem("tab0"), 16)
            e.dma_start(nrows(tab_edge_a), H).then_inc(sem("tab_a"), 16)
            lane_start_sync(e, 0)
            for r in range(R):
                load_fill(e, 0, 0, r)
            with e.Fori(1, ITERS) as i:
                for r in range(R):
                    pass_index(e, 0, i, r)
                    load_fill(e, 0, i, r)
            for l, table in ((1, tab_gcn), (2, tab_hop1), (3, tab_hop2)):
                store_table(e, l, table)

                def body(i):
                    for r in range(R):
                        pass_index(e, l, i, r)
                loop(e, body)
                if l == 2:
                    e.wait_ge(sem("fill_clear"), 2)
                    for a in accs:
                        e.dma_start(a.rearrange("(p t) f -> p t f", p=P),
                                    fill[:, :, :, :].rearrange("p r k f -> p (r k) f")[:, 0:TILES + 1, :])\
                            .then_inc(sem("acc_zeroed"), 16)
            e.wait_ge(sem("acc_zeroed"), 16 * len(accs))
            store_table(e, 4, tab_last)
            lane_start_sync(e, 1)

            def body4(i):
                for r in range(R):
                    wait(e, "messages", (i * R + (r - R + 1)) * NL)
                    gate(e)
                    load_fill(e, 4, i, r)
                    e.dma_start(idx[:, r, :], src_l[:, bass.ds((i * R + r) * K, K)]).then_inc(sem(f"first4_{r}"), 16)
                    e.dma_start(wblk[:, r, :], w_l[:, bass.ds((i * R + r) * K, K)]).then_inc(sem(f"first4_{r}"), 16)
            loop(e, body4)
            for s in range(ACC_SETS):
                e.wait_ge(sem(f"added{s}"), 16 * ACC_PER_SET * SET_GROUPS[s] * ITERS)
            for g in range(NGROUPS):
                ts = slice(g * NT, (g + 1) * NT)
                wait(e, "aggregated", 3 * NGROUPS + g - 1)
                for k, a in enumerate(accs):
                    e.dma_start(acc_buf(g, k), nrows(a[0:ROWS, :])[:, ts, :]).then_inc(sem(f"acc_in{g % 2}"), 16)
            e.wait_ge(sem("x_final"), 1)
            e.dma_start(out[0:(P - 1) * TILES, :].rearrange("(p t) f -> p t f", t=TILES), X[0:P - 1, :, :])\
                .then_inc(sem("x_out"), 16)
            e.dma_start(out[(P - 1) * TILES:N, :].rearrange("(p t) f -> p t f", p=1), X[P - 1:P, 0:LAST_ROWS, :])\
                .then_inc(sem("x_out"), 16)
            e.wait_ge(sem("x_out"), 32)

        @block.gpsimd
        def _(e):
            chain = Chain(e, "g_chain")
            chain(e.memset(ident[:, :], 0.0))
            chain(e.memset(before[:, :], 1.0))
            chain(e.memset(earlier[:, :], 1.0))
            chain(e.affine_select(out=ident[:, :], in_=ident[:, :], compare_op=ALU.not_equal, fill=1.0,
                                  base=0, pattern=[[-1, P]], channel_multiplier=1))
            chain(e.affine_select(out=before[:, :], in_=before[:, :], compare_op=ALU.is_gt, fill=0.0,
                                  base=0, pattern=[[1, P]], channel_multiplier=-1))
            chain(e.affine_select(out=earlier[:, :], in_=earlier[:, :], compare_op=ALU.is_gt, fill=0.0,
                                  base=0, pattern=[[-1, P]], channel_multiplier=1))
            chain(e.iota(iota_i[:, :], pattern=[[1, P]], base=0, channel_multiplier=0))
            chain(e.iota(colp_i[:, 0:1], pattern=[[0, 1]], base=0, channel_multiplier=LANE))
            chain(e.iota(colp_i[:, 1:2], pattern=[[0, 1]], base=ROWS, channel_multiplier=1))
            chain(e.memset(prev_i[:, :], -1))
            chain(e.iota(node_i[:, :], pattern=[[1, TILES + 1]], base=0, channel_multiplier=TILES))
            e.sem_inc(sem("const"), 1)
            e.wait_ge(sem("chunked"), 1)
            for t in range(TILES + 1):
                e.indirect_dma_start(out=chunks[:, t, 0:CHUNK].bitcast(i32), out_offset=None,
                                     in_=dst.rearrange("(c k) -> c k", k=CHUNK),
                                     in_offset=bass.IndirectOffsetOnAxis(ap=chunk_i[:, t:t + 1], axis=0))\
                    .then_inc(sem("chunks_in"), 16)
            e.wait_ge(sem("tab0"), 16 * NGROUPS)
            e.wait_ge(sem("placeable"), 1)
            for r in range(R):
                gather_slot(e, 0, 0, r, tab_edge_b)
            e.wait_ge(sem("tab_a"), 16)
            e.wait_ge(sem("zeroed"), 16 * (LANE // (R * K)))
            first_rows_gpsimd(e, 0, tab_edge_a)
            with e.Fori(1, ITERS) as i:
                for r in range(R):
                    gather_slot(e, 0, i, r, tab_edge_b)
            fix_gpsimd(e, 0)
            for l, table in ((1, tab_gcn), (2, tab_hop1), (3, tab_hop2)):
                e.wait_ge(sem(f"tab{l}"), 16 * NGROUPS)

                def body(i):
                    for r in range(R):
                        gather_slot(e, l, i, r, table)
                loop(e, body)
                fix_gpsimd(e, l)
            e.wait_ge(sem("tab4"), 16 * NGROUPS)
            first_rows_gpsimd(e, 1, tab_last)
            e.wait_ge(sem("acc_zeroed"), 16 * len(accs))

            def body4(i):
                for r in range(R):
                    wait(e, "messages", (i * R + r) * NL + NL)
                    wait(e, "targets", i * R + (r + 1))
                    gate(e)
                    for g in range(K // ACC_PER_SET):
                        G = r * (K // ACC_PER_SET) + g
                        s = G % ACC_SETS
                        n = i * SET_GROUPS[s] + G // ACC_SETS
                        if not (isinstance(n, int) and n == 0):
                            wait(e, f"added{s}", n * (16 * ACC_PER_SET))
                            gate(e)
                        for a in range(ACC_PER_SET):
                            j = g * ACC_PER_SET + a
                            e.indirect_dma_start(
                                out=accs[s * ACC_PER_SET + a][:, :],
                                out_offset=bass.IndirectOffsetOnAxis(ap=idx2[:, r, j:j + 1], axis=0),
                                in_=ring[:, r, j, :], in_offset=None, compute_op=ALU.add)\
                                .then_inc(sem(f"added{s}"), 16)
            loop(e, body4)

        @block.vector
        def _(e):
            chain = Chain(e, "v_chain")
            e.memset(fill[:, :, :, :], 0.0).then_inc(sem("fill_clear"), 1)
            e.memset(X[96:P, :, :], 0.0).then_inc(sem("x_padded"), 1)
            e.memset(w_diag[:, :], 0.0).then_inc(sem("diag_clear"), 1)
            chain(e.memset(zero_row[:, :], 0.0))
            e.wait_ge(sem("const"), 1)
            chain(e.tensor_copy(iota_b[:, :], iota_i[:, :]))
            chain(e.tensor_copy(lane0[:, :], colp_i[:, 0:1]))
            chain(e.tensor_copy(spare[:, :], colp_i[:, 1:2]))
            chain(e.memset(ones[:, :], 1.0))
            chain(e.memset(carryT[:, :], 0.0))
            chain(e.memset(eps[:, :], 1e-5))
            chain(e.tensor_copy(node_f[:, :], node_i[:, :]))
            def take_ab(p, t, n):
                e.tensor_tensor(H[:, t:t + n, :], p[:, :, 0:D], brow3(bias["e1"][:, :], n), ALU.add)
                return e.tensor_copy(M[:, t:t + n, :], p[:, :, D:2 * D])
            e.wait_ge(sem("dst_in"), 32)
            chain(e.tensor_copy(first_i[:, :], keep[:, 0:1].bitcast(i32)))
            chain(e.tensor_copy(dst_f[:, :], keep[:, :].bitcast(i32)))
            chain(e.tensor_copy(col["first"][:, :], first_i[:, :]))
            chain(e.tensor_copy(col["prev"][:, :], prev_i[:, :]))
            chain(e.tensor_tensor(keep[:, 1:LANE], dst_f[:, 1:LANE], dst_f[:, 0:LANE - 1], ALU.is_equal))
            chain(e.memset(keep[:, 0:1], 0.0))
            loop_chain = Chain(e, "v_loop")
            chain(e.tensor_copy(pivot[:, :], dst_f[:, 0:LANE:CHUNK]))
            divide(e, chain, pivot[:, :], PIVOTS)
            onehots(e, "hd", 0, PGRP)
            e.wait_ge(sem("hd_used"), PGRP)
            chain(e.tensor_scalar(oh_q[:, :, :, :].rearrange("p a b c -> p (a b c)")[:, 0:LANE], dst_f[:, :], col["first"][:, 0:1], 0.0, ALU.is_equal, ALU.add,
                                  accum_out=col["cnt"][:, :]))
            chain(e.tensor_scalar(limit[:, :], keep[:, :], 2.0, -1.0, ALU.mult, ALU.add))
            chain(e.tensor_scalar(limit[:, :], limit[:, :], FULL, None, ALU.mult))
            chain(e.scalar_tensor_tensor(out=fix_i[:, :], in0=col["cnt"][:, :], scalar=-1.0, in1=lane0[:, :],
                                         op0=ALU.add, op1=ALU.add))
            chain(e.tensor_tensor(col["cont"][:, :], col["first"][:, :], col["prev"][:, :], ALU.is_equal))
            chain(e.tensor_scalar(col["whole"][:, :], col["cnt"][:, :], float(LANE), None, ALU.is_equal))
            chain(e.tensor_tensor(col["k"][:, :], col["whole"][:, :], col["cont"][:, :], ALU.mult))
            chain(e.tensor_scalar(col["contL"][:, :], col["cont"][:, :], 2.0, -1.0, ALU.mult, ALU.add))
            chain(e.tensor_scalar(col["contL"][:, :], col["contL"][:, :], FULL, None, ALU.mult))
            chain(e.tensor_tensor_scan(out=stat["incl"][:, :], data0=ones[:, :], data1=hist[:, :],
                                       initial=0.0, op0=ALU.mult, op1=ALU.add))
            chain(e.tensor_copy(col["tot"][:, :], stat["incl"][:, TILES - 1:TILES]))
            e.sem_inc(sem("counted"), 1)
            e.wait_ge(sem("offset"), 1)
            chain(e.tensor_copy(col["offs"][:, :], pa[:, 0:1]))
            chain(e.tensor_copy(krow[:, :], pb[0:D, :]))
            chain(e.tensor_scalar(krowL[:, :], krow[:, :], 2.0, -1.0, ALU.mult, ALU.add))
            chain(e.tensor_scalar(krowL[:, :], krowL[:, :], FULL, None, ALU.mult))
            chain(e.tensor_copy(chunk_f[:, 0:1], col["offs"][:, :]))
            chain(e.tensor_scalar(chunk_f[:, 1:TILES + 1], stat["incl"][:, :], col["offs"][:, 0:1], None, ALU.add))
            chain(e.tensor_scalar(chunk_f[:, :], chunk_f[:, :], -1.0, 0.0, ALU.add, ALU.max))
            chain(e.tensor_copy(chunk_i[:, :], chunk_f[:, :]))
            e.sem_inc(sem("chunked"), 1)
            def place_nodes():
                e.wait_ge(sem("chunks_in"), 16 * (TILES + 1))
                mc = chunks[:, 0:TILES + 1, 0:CHUNK]
                chain(e.tensor_tensor(mc, mc.bitcast(i32), bcast(node_f[:, :], CHUNK), ALU.is_lt))
                chain(e.tensor_reduce(out=edge0[:, :], in_=mc, op=ALU.add, axis=AX.X))
                chain(e.scalar_tensor_tensor(out=edge0[:, :], in0=chunk_f[:, :], scalar=float(CHUNK), in1=edge0[:, :],
                                             op0=ALU.mult, op1=ALU.add))
                chain(e.tensor_tensor(stat["deg"][:, :], edge0[:, 1:TILES + 1], edge0[:, 0:TILES], ALU.subtract))
                chain(e.tensor_scalar(stat["has"][:, :], stat["deg"][:, :], 0.0, None, ALU.is_gt))
                chain(e.tensor_scalar(stat["tmp"][:, :], stat["has"][:, :], -BEYOND, BEYOND, ALU.mult, ALU.add))
                chain(e.tensor_tensor(start_i[:, :], stat["tmp"][:, :], edge0[:, 0:TILES], ALU.add))
                chain(e.scalar_tensor_tensor(out=end_i[:, :], in0=stat["tmp"][:, :], scalar=-1.0,
                                             in1=edge0[:, 1:TILES + 1], op0=ALU.add, op1=ALU.add))
                e.sem_inc(sem("placeable"), 1)
                chain(e.tensor_scalar(stat["deg"][:, :], stat["deg"][:, :], 1.0, None, ALU.max))
                chain(e.reciprocal(stat["inv"][:, :], stat["deg"][:, :]))
                e.sem_inc(sem("degrees"), 1)

            e.wait_ge(sem("w_in"), 16 * 16)
            chain(e.tensor_tensor(w_ab[:, 0:D], w_ab[:, 0:D], w_ab[:, D:2 * D], ALU.subtract))
            chain(e.tensor_tensor(bias["last"][:, :], bias["last"][:, :], bias["last2"][:, :], ALU.add))
            e.wait_ge(sem("x_in"), 32)
            for g in range(NGROUPS + 1):
                if g < NGROUPS:
                    norm_vector(e, chain, 0, g)
                    e.sem_inc(sem("normed"), 1)
                if g == NGROUPS - 2:
                    place_nodes()
                if g:
                    mm_vector(e, "ab", g - 1, 2 * D, take_ab)
                    e.sem_inc(sem("ab_made"), 1)

            def body0(i):
                for r in range(R):
                    b = i * R + r
                    load_masks(e, loop_chain, i, r)
                    loop_chain(e.tensor_copy(mblk[:, 1, :], limit[:, bass.ds(b * K, K)]))
                    wait(e, f"first0_{r}", i * 16 + 16)
                    scan_columns(e, loop_chain, fill, b, r, mblk[:, 0, :], ALU.mult, ALU.add, range(K))
                    e.sem_inc(sem("filled0"), 1)
                    wait(e, f"gathered0_{r}", i * (16 * K) + 16 * K)
                    loop_chain(e.tensor_tensor(ring[:, r, :, :], ring[:, r, :, :], fill[:, r, :, :], ALU.add))
                    e.sem_inc(sem("summed0"), 1)
                    loop_chain(e.tensor_copy(srcf[:, :], idx[:, r, :]))
                    divide(e, loop_chain, srcf[:, :], K)
                    onehots(e, "hs", b * (K // HG), K // HG)
                    for q, cols in enumerate(MAXQ):
                        wait(e, "products0", b * NQ + (q + 1))
                        scan_columns(e, loop_chain, ring, b, r, mblk[:, 1, :], ALU.min, ALU.max, cols, om[q % 2])
                        e.sem_inc(sem("taken0"), 1)
                    loop_chain.clear()
                    e.sem_inc(sem("scanned"), 1)
            e.wait_ge(sem("tab0"), 16 * NGROUPS)
            chain(e.memset(M, 0.0))
            e.sem_inc(sem("cleared"), 1)
            loop(e, body0)
            fix_vector(e, chain, 0, ALU.min, ALU.max, krowL, col["contL"])
            e.wait_ge(sem("hs_used"), LANE // HG)
            chain(e.tensor_scalar(stat["nsrc"][:, :], hist[:, :], 1.0, None, ALU.max))
            e.sem_inc(sem("degrees"), 1)
            e.wait_ge(sem("rooted"), 2)
            chain(e.reciprocal(stat["nsrc"][:, :], stat["nsrc"][:, :]))
            chain(e.reciprocal(stat["ndst"][:, :], stat["ndst"][:, :]))
            for g in range(NGROUPS):
                ts = slice(g * NT, (g + 1) * NT)
                h, m, xs = H[:, ts, :], M[:, ts, :], X[:, ts, :]
                e.wait_ge(sem(f"node_rows{g}"), 16 * NT)
                chain(e.tensor_tensor(m, m, brow3(bias["e2"][:, :], NT), ALU.add))
                chain(e.tensor_tensor(h, m, m, ALU.subtract))
                chain(e.scalar_tensor_tensor(out=h.bitcast(i32), in0=h, scalar=0.0, in1=bcast(stat["has"][:, ts]),
                                             op0=ALU.is_equal, op1=ALU.mult))
                chain(e.tensor_tensor(m, m, xs, ALU.add))
                chain(e.copy_predicated(xs, h.bitcast(i32), m))
                norm_vector(e, chain, 1, g)
                chain(e.tensor_tensor(h, h, bcast(stat["nsrc"][:, ts]), ALU.mult))
                e.sem_inc(sem("table_made"), 1)
            sum_pass_vector(e, 1)

            def take_gcn(p, t, n):
                h, xs = H[:, t:t + n, :], X[:, t:t + n, :]
                chain(e.tensor_tensor(h, p, brow3(bias["gcn"][:, :], n), ALU.add))
                chain(e.scalar_tensor_tensor(out=h, in0=h, scalar=0.01, in1=h, op0=ALU.mult, op1=ALU.max))
                return e.tensor_tensor(xs, xs, h, ALU.add)

            def take_hop1(p, t, n):
                h = H[:, t:t + n, :]
                chain(e.tensor_tensor(h, p, brow3(bias["hop1"][:, :], n), ALU.add))
                return e.tensor_scalar(h, h, 0.0, None, ALU.max)

            def take_add(name):
                def take(p, t, n):
                    h, xs = H[:, t:t + n, :], X[:, t:t + n, :]
                    chain(e.tensor_tensor(h, p, brow3(bias[name][:, :], n), ALU.add))
                    return e.tensor_tensor(xs, xs, h, ALU.add)
                return take

            def nodes(l, name, factor, take, norm):
                fix_vector(e, chain, l, ALU.mult, ALU.add, krow, col["cont"])
                for g in range(NGROUPS + 1):
                    if g < NGROUPS:
                        ts = slice(g * NT, (g + 1) * NT)
                        e.wait_ge(sem(f"node_rows{g}"), 16 * NT * (l + 1))
                        chain(e.tensor_tensor(M[:, ts, :], M[:, ts, :], bcast(stat[factor][:, ts]), ALU.mult))
                        e.sem_inc(sem("aggregated"), 1)
                    if g:
                        mm_vector(e, name, g - 1, D, take)
                        if norm is not None:
                            norm_vector(e, chain, norm, g - 1)
                        e.sem_inc(sem("table_made"), 1)
            nodes(1, "gcn", "ndst", take_gcn, 2)
            sum_pass_vector(e, 2)
            nodes(2, "hop1", "inv", take_hop1, None)
            sum_pass_vector(e, 3)
            nodes(3, "hop2", "inv", take_add("hop2"), 3)
            e.wait_ge(sem("w_turned"), 1)
            chain(e.tensor_copy(w_last[:, :], pa[:, 0:D]))
            e.sem_inc(sem("w_copied"), 1)

            def body4(i):
                for r in range(R):
                    b = i * R + r
                    load_masks(e, loop_chain, i, r)
                    wait(e, f"first4_{r}", i * 48 + 48)
                    loop_chain(e.tensor_copy(srcf[:, :], idx[:, r, :]))
                    e.sem_inc(sem("numbered"), 1)
                    scan_columns(e, loop_chain, fill, b, r, mblk[:, 0, :], ALU.mult, ALU.add, range(K))
                    e.sem_inc(sem("filled4"), 1)
                    for q, cols in enumerate(LASTQ):
                        g = b * NL + q
                        wait(e, "spread", g + 1)
                        wait(e, "products4", b * NL + (q + 1 - back(q)))
                        wait(e, "matched", b * NL + (q + 1 - back(q)))
                        for k, j in enumerate(cols):
                            row = tp[q % 2][:, k * P:(k + 1) * P]
                            e.tensor_scalar(eqw[:, q % 2, k, :], row, srcf[:, j:j + 1], wblk[:, r, j:j + 1],
                                            ALU.is_equal, ALU.mult)
                            last = e.scalar_tensor_tensor(out=dupjunk[:, q % 2, k, :], in0=row, scalar=srcf[:, j:j + 1],
                                                          in1=earlier[:, :], op0=ALU.is_equal, op1=ALU.mult,
                                                          accum_out=dupc[:, j:j + 1])
                        last.then_inc(sem("matched"), 1)
                    wait(e, "matched", b * NL + NL)
                    loop_chain(e.tensor_scalar(dup1[:, :], dupc[:, :], 0.0, None, ALU.is_gt))
                    loop_chain(e.tensor_scalar(dup2[:, :], srcf[:, :], -1.0, spare[:, 0:1], ALU.mult, ALU.add))
                    loop_chain(e.tensor_tensor(dup2[:, :], dup2[:, :], dup1[:, :], ALU.mult))
                    wait_slot_added(e, i, r)
                    loop_chain(e.tensor_tensor(idx2[:, r, :], dup2[:, :], srcf[:, :], ALU.add))
                    loop_chain.clear()
                    e.sem_inc(sem("targets"), 1)
            loop(e, body4)
            for g in range(NGROUPS + 1):
                if g < NGROUPS:
                    m = M[:, g * NT:(g + 1) * NT, :]
                    e.wait_ge(sem(f"acc_in{g % 2}"), 16 * len(accs) * (g // 2 + 1))
                    chain(e.tensor_tensor(m, acc_buf(g, 0), acc_buf(g, 1), ALU.add))
                    for k in range(2, len(accs)):
                        chain(e.tensor_tensor(m, m, acc_buf(g, k), ALU.add))
                    e.sem_inc(sem("aggregated"), 1)
                if g:
                    mm_vector(e, "last", g - 1, D, take_add("last"))
            e.sem_inc(sem("x_final"), 1)

        @block.scalar
        def _(e):
            zero = fill[:, :, :, :].rearrange("p r k f -> p (r k) f")
            firsts = iter(range(0, LANE, R * K))

            def zero_part(c):
                e.dma_start(lrows(first_rows)[:, c:c + R * K, :], zero).then_inc(sem("zeroed"), 16)
            e.wait_ge(sem("fill_clear"), 1)
            e.wait_ge(sem("x_in"), 32)
            for _ in range(4):
                zero_part(next(firsts))
            for g in range(NGROUPS + 1):
                if g < NGROUPS:
                    norm_scalar(e, 0, g)
                    if g < NGROUPS - 2:
                        zero_part(next(firsts))
                if g:
                    mm_scalar(e, "ab", g - 1, D)
            e.wait_ge(sem("tab0"), 16 * NGROUPS)
            for c in firsts:
                zero_part(c)
            e.wait_ge(sem("degrees"), 1)
            e.activation(stat["ndst"][:, :], stat["deg"][:, :], ACT.Sqrt).then_inc(sem("rooted"), 1)

            def body0(i):
                for r in range(R):
                    b = i * R + r
                    wait(e, "summed0", b + 1)
                    e.activation(ring[:, r, :, :], ring[:, r, :, :], ACT.Relu).then_inc(sem("relued0"), 1)
                    for q, cols in enumerate(MAXQ):
                        rows, w = (P, len(cols) // 2 * P) if len(cols) > 1 else (D, P)
                        wait(e, "turned0", b * NQ + (q + 1))
                        wait(e, "products0", b * NQ + (q - 1))
                        e.activation(hT[0:rows, q % 2, 0:w], tp[q % 2][0:rows, 0:w], ACT.Copy)\
                            .then_inc(sem("copied0"), 1)
                    pass_store(e, 0, i, r)
            loop(e, body0)
            e.wait_ge(sem("degrees"), 2)
            e.activation(stat["nsrc"][:, :], stat["nsrc"][:, :], ACT.Sqrt).then_inc(sem("rooted"), 1)
            for g in range(NGROUPS):
                norm_scalar(e, 1, g)
            for l, name, kd, norm in ((1, "gcn", D, 2), (2, "hop1", 2 * D, None), (3, "hop2", 2 * D, 3)):
                def body(i):
                    for r in range(R):
                        pass_store(e, l, i, r)
                loop(e, body)
                for g in range(NGROUPS):
                    mm_scalar(e, name, g, kd)
                    if norm is not None:
                        norm_scalar(e, norm, g)

            def body4(i):
                for r in range(R):
                    b = i * R + r
                    wait_slot_added(e, i, r)
                    for q, cols in enumerate(LASTQ):
                        wait(e, "products4", b * NL + (q + 1))
                        e.activation(ring[:, r, cols[0]:cols[-1] + 1, :],
                                     om[q % 2][:, 0:len(cols) * D].rearrange("p (k f) -> p k f", f=D), ACT.Copy)\
                            .then_inc(sem("messages"), 1)
            loop(e, body4)
            for g in range(NGROUPS):
                mm_scalar(e, "last", g, 2 * D)

        @block.tensor
        def _(e):
            e.wait_ge(sem("const"), 1)
            count_tensor(e, "hd", 0, PGRP, True)
            e.wait_ge(sem("counted"), 1)
            e.matmul(pa[:, 0:1], before[:, :], col["tot"][:, :], start=True, stop=True)
            e.matmul(pb[0:D, :], col["k"][:, 0:1].broadcast_to([P, D]), ident[:, :], start=True, stop=True)\
                .then_inc(sem("offset"), 1)
            for g in range(NGROUPS):
                e.wait_ge(sem("normed"), g + 1)
                mm_tensor(e, "ab", g, 0, D, w_ab[:, :], 2 * D)
            e.wait_ge(sem("placeable"), 1)

            def body0(i):
                for r in range(R):
                    b = i * R + r
                    wait(e, "relued0", b + 1)
                    for q, cols in enumerate(MAXQ):
                        wait(e, "copied0", b * NQ + (q - 1))
                        gate(e)
                        for k, c in enumerate(pairs(cols)):
                            m = len(c) * D
                            last = e.transpose(tp[q % 2][0:m, k * P:(k + 1) * P],
                                               ring[:, r, c[0]:c[-1] + 1, :], ident[:, :])
                        last.then_inc(sem("turned0"), 1)
                        wait(e, "copied0", b * NQ + (q + 1))
                        wait(e, "taken0", b * NQ + (q - 1))
                        for k, c in enumerate(pairs(cols)):
                            m = len(c) * D
                            last = e.matmul(om[q % 2][:, k * P:k * P + m], hT[0:m, q % 2, k * P:(k + 1) * P],
                                            w_diag[0:m, 0:m], start=True, stop=True)
                        last.then_inc(sem("products0"), 1)
                    count_tensor(e, "hs", b * (K // HG), K // HG, isinstance(i, int) and r == 0)
            loop(e, body0)
            fix_tensor(e, 0)
            for l, name, c0, rhs in ((1, "gcn", D, w_gcn), (2, "hop1", 0, w_hop1), (3, "hop2", 0, w_hop2)):
                fix_tensor(e, l)
                for g in range(NGROUPS):
                    e.wait_ge(sem("aggregated"), (l - 1) * NGROUPS + g + 1)
                    mm_tensor(e, name, g, c0, 2 * D, rhs[:, :], D)
            e.transpose(pa[:, 0:D], w_lastT[:, :], ident[0:D, 0:D]).then_inc(sem("w_turned"), 1)

            def spread(b, q, cols):
                wait(e, "matched", b * NL + (q + 1 - back(q)))
                for k, j in enumerate(cols):
                    last = e.matmul(tp[q % 2][:, k * P:(k + 1) * P], srcf[:, j:j + 1].broadcast_to([P, P]),
                                    ident[:, :], start=True, stop=True)
                last.then_inc(sem("spread"), 1)

            def body4(i):
                for r in range(R):
                    b = i * R + r
                    wait(e, "numbered", b + 1)
                    spread(b, 0, LASTQ[0])
                    for q, cols in enumerate(LASTQ):
                        if q + 1 < NL:
                            spread(b, q + 1, LASTQ[q + 1])
                        if q == 0:
                            wait(e, "filled4", b + 1)
                        wait(e, "matched", b * NL + (q + 1))
                        wait(e, "messages", b * NL + (q + 1 - back(q)))
                        for k, j in enumerate(cols):
                            last = e.matmul(om[q % 2][:, k * D:(k + 1) * D], eqw[:, q % 2, k, :],
                                            fill[:, r, j, :], start=True, stop=True)
                        last.then_inc(sem("products4"), 1)
            loop(e, body4)
            e.wait_ge(sem("w_copied"), 1)
            for g in range(NGROUPS):
                e.wait_ge(sem("aggregated"), 3 * NGROUPS + g + 1)
                mm_tensor(e, "last", g, 0, 2 * D, w_last[:, :], D)


_INS = ["x", "src", "dst", "edge_weight", "L0_gnn_W1", "L0_gnn_b1", "L0_gnn_W2", "L0_gnn_b2", "L1_gnn_W",
        "L1_gnn_b", "L2_gnn_W1", "L2_gnn_b1", "L2_gnn_W2", "L2_gnn_b2", "L3_gnn_W_self", "L3_gnn_b_self",
        "L3_gnn_W_neigh", "L3_gnn_b_neigh"]


def kernel(**inputs):
    import numpy as _np
    import concourse.bacc as _bacc
    from concourse import mybir as _mybir
    from concourse.bass_utils import run_bass_kernel_spmd as _run

    nc = _bacc.Bacc("TRN2", target_bir_lowering=False, num_devices=1)
    arrays, args = {}, []
    for name in _INS:
        a = _np.ascontiguousarray(inputs[name])
        arrays["in_" + name] = a
        args.append(nc.dram_tensor("in_" + name, a.shape, _mybir.dt.from_np(a.dtype), kind="ExternalInput").ap())
    args.append(nc.dram_tensor("out_0", (N, D), _mybir.dt.float32, kind="ExternalOutput").ap())
    build(nc, *args)
    return _run(nc, [arrays], core_ids=[0]).results[0]["out_0"]
```

```python
import concourse.bass as bass
from concourse import mybir
from contextlib import ExitStack

N, E, D = 12500, 400000, 64
P = 128
TILES = -(-N // P)
ROWS = P * TILES
LANE = E // P
K = 25
R = 5
BLOCKS = LANE // K
ITERS = BLOCKS // R
HG = 5
HBUF = 5
ZERO_FIRST, ZERO_BETWEEN = 7, 4
AHEAD = 3
CHUNK = 25
PIVOTS = LANE // CHUNK
NT = 7
NGROUPS = TILES // NT
ACC_SETS, ACC_PER_SET = 2, 5
FULL = 3.4028234663852886e38
LAST_ROWS = N - (P - 1) * TILES
BEYOND = 2.0 * E


def build(nc, x, src, dst, edge_weight, l0_w1, l0_b1, l0_w2, l0_b2, l1_w, l1_b,
          l2_w1, l2_b1, l2_w2, l2_b2, l3_ws, l3_bs, l3_wn, l3_bn, out):
    f32, bf16, i32 = mybir.dt.float32, mybir.dt.bfloat16, mybir.dt.int32
    ALU, ACT, AX = mybir.AluOpType, mybir.ActivationFunctionType, mybir.AxisListType
    assert N <= ROWS and E == P * LANE and LANE == K * R * ITERS and BLOCKS == R * ITERS
    ctx = ExitStack()
    with ctx:
        def sb(name, shape, dt=f32):
            return ctx.enter_context(nc.sbuf_tensor(name, shape, dt))

        def ps(name, shape):
            return ctx.enter_context(nc.psum_tensor(name, shape, f32))

        sems = {}

        def sem(name):
            if name not in sems:
                sems[name] = ctx.enter_context(nc.semaphore(name))
            return sems[name]

        def dram(name, shape, dt=f32):
            return nc.dram_tensor(name, shape, dt).ap()

        tab_edge_a = dram("tab_edge_a", (ROWS, D))
        tab_edge_b = dram("tab_edge_b", (ROWS, D))
        tab_gcn = dram("tab_gcn", (ROWS, D))
        tab_hop1 = dram("tab_hop1", (ROWS, D))
        tab_hop2 = dram("tab_hop2", (ROWS, D))
        tab_last = dram("tab_last", (ROWS, D))
        edge_rows = dram("edge_rows", (E, D))
        first_rows = dram("first_rows", (E, D))
        accs = [dram(f"acc{k}", (ROWS + P, D)) for k in range(ACC_SETS * ACC_PER_SET)]

        e_src, e_dst = dram("e_src", (E, 1), i32), dram("e_dst", (E, 1), i32)
        e_weight = dram("e_weight", (E, 1))
        places = dram("places", (ROWS + P, 1))

        X = sb("X", [P, TILES, D])
        HM = sb("HM", [P, TILES, 2 * D])
        H, M = HM[:, :, 0:D], HM[:, :, D:2 * D]
        dst_f = sb("dst_f", [P, LANE])
        limit = dst_f
        keep = sb("keep", [P, LANE])
        ring = sb("ring", [P, R, K, D])
        fill = sb("fill", [P, R, K, D])
        idx = sb("idx", [P, R, K], i32)
        idx2 = sb("idx2", [P, R, K], i32)
        wblk = sb("wblk", [P, R, K])
        mblk = sb("mblk", [P, 2, K])
        srcf = sb("srcf", [P, K])
        dupc = sb("dupc", [P, K])
        dup1 = sb("dup1", [P, K])
        dup2 = sb("dup2", [P, K])
        dupjunk = sb("dupjunk", [P, 2, 4, P], bf16)
        hT = sb("hT", [P, 2, 512])
        eqw = sb("eqw", [P, 2, 4, P])
        oh_q = sb("oh_q", [P, HBUF, HG, P], bf16)
        oh_r = sb("oh_r", [P, HBUF, HG, TILES], bf16)
        hq, hr, ht = (sb(n, [P, PIVOTS]) for n in ("hq", "hr", "ht"))
        hi = sb("hi", [P, PIVOTS], i32)
        pivot = sb("pivot", [P, PIVOTS])
        ident = sb("ident", [P, P])
        before = sb("before", [P, P])
        earlier = sb("earlier", [P, P])
        iota_i = sb("iota_i", [P, P], i32)
        iota_b = sb("iota_b", [P, P], bf16)
        colp_i = sb("colp_i", [P, 2], i32)
        lane0 = sb("lane0", [P, 1])
        spare = sb("spare", [P, 1])
        ones = sb("ones", [P, TILES])
        w_ab = sb("w_ab", [D, 2 * D])
        w_diag = sb("w_diag", [P, P])
        w_gcn = sb("w_gcn", [D, D])
        w_hop1 = sb("w_hop1", [P, D])
        w_hop2 = sb("w_hop2", [P, D])
        node_f = sb("node_f", [P, TILES + 1])
        node_i = sb("node_i", [P, TILES + 1], i32)
        chunk_f = sb("chunk_f", [P, TILES + 1])
        chunk_i = sb("chunk_i", [P, TILES + 1], i32)
        edge0 = sb("edge0", [P, TILES + 1])
        w_lastT = sb("w_lastT", [D, 2 * D])
        w_last = sb("w_last", [P, D])
        bias = {n: sb("bias_" + n, [P, D]) for n in ("e1", "e2", "gcn", "hop1", "hop2", "last", "last2")}
        stat = {n: sb("stat_" + n, [P, TILES]) for n in
                ("mean", "var", "rstd", "deg", "has", "incl", "nsrc", "ndst", "inv", "tmp")}
        eps = sb("eps", [P, 1])
        start_i = sb("start_i", [P, TILES], i32)
        end_i = sb("end_i", [P, TILES], i32)
        fix_i = sb("fix_i", [P, 1], i32)
        first_i = sb("first_i", [P, 1], i32)
        prev_i = sb("prev_i", [P, 1], i32)
        col = {n: sb("col_" + n, [P, 1]) for n in
               ("first", "prev", "cnt", "cont", "whole", "k", "contL", "offs", "tot")}
        krow = sb("krow", [D, P])
        krowL = sb("krowL", [D, P])
        carryT = sb("carryT", [D, P + 1])
        tail = sb("tail", [P, D])
        fixrow = sb("fixrow", [P, D])
        zero_row = sb("zero_row", [P, D])
        lane_init = sb("lane_init", [P, D])

        bad = sb("bad", [P, 2])
        bad_i = sb("bad_i", [1, 1], i32)
        c_dst, c_src = sb("c_dst", [P, 1], i32), sb("c_src", [P, 1], i32)
        c_w, c_dst_f, c_next, c_rank, c_after, c_new, c_step = (
            sb(n, [P, 1]) for n in ("c_w", "c_dst_f", "c_next", "c_rank", "c_after", "c_new", "c_step"))
        c_pos, c_home = sb("c_pos", [P, 1], i32), sb("c_home", [P, 1], i32)
        match = sb("match", [P, 2, P], bf16)

        tp = [ps(f"tp{k}", [P, 512]) for k in range(2)]
        om = [ps(f"om{k}", [P, 512]) for k in range(2)]
        hist = ps("hist", [P, TILES])
        pa = ps("pa", [P, P])
        pb = ps("pb", [P, P])

        oh_flat = oh_q[:, :, :, :].rearrange("p a b c -> p (a b c)")
        chunks = ring[:, :, :, :].rearrange("p r k f -> p (r k) f")

        lanes = lambda a: a.rearrange("(p c) -> p c", p=P)
        lrows = lambda a: a.rearrange("(p c) f -> p c f", p=P)
        nrows = lambda a: a.rearrange("(p t) f -> p t f", p=P)
        lanes1 = lambda a: a.rearrange("(p c) o -> p (c o)", p=P)
        src_l, dst_l, w_l = lanes1(e_src), lanes1(e_dst), lanes1(e_weight)
        brow = lambda b: b.rearrange("(a n) -> a n", a=1).partition_broadcast(P)

        def wait(e, name, n):
            if not (isinstance(n, int) and n <= 0):
                e.wait_ge(sem(name), n)

        def gate(e):
            e.sem_inc(sem("gate_" + e.engine.name), 1)

        def loop(e, body):
            body(0)
            with e.Fori(1, ITERS) as i:
                body(i)

        class Chain:
            def __init__(self, e, name):
                self.e, self.name, self.n = e, name, 0

            def __call__(self, ins, meanwhile=iter(())):
                self.n += 1
                ins.then_inc(sem(self.name), 1)
                next(meanwhile, None)
                self.e.wait_ge(sem(self.name), self.n)

            def clear(self):
                self.e.sem_clear(sem(self.name))
                self.n = 0

        def bcast(ap2, n=D):
            return ap2.unsqueeze(2).broadcast_to([P, ap2.shape[1], n])

        def brow3(b, n):
            return b.unsqueeze(1).broadcast_to([P, n, D])

        SUB = [range(a, min(a + 4, NT)) for a in range(0, NT, 4)]
        assert len(SUB) % 2 == 0 and TILES == NT * NGROUPS
        MM = {n: k * NGROUPS * len(SUB) for k, n in enumerate(("ab", "gcn", "hop1", "hop2", "last"))}

        def batches(name, g):
            return [(MM[name] + g * len(SUB) + q, q % 2, [g * NT + t for t in ts]) for q, ts in enumerate(SUB)]

        def mm_tensor(e, name, g, c0, c1, rhs, m):
            kd = c1 - c0
            for n, u, ts in batches(name, g):
                wait(e, "mm_copied", n - 1)
                for k, t in enumerate(ts):
                    last = e.transpose(tp[u][0:kd, k * P:(k + 1) * P], HM[:, t, c0:c1], ident[:, :])
                last.then_inc(sem("mm_turned"), 1)
                wait(e, "mm_copied", n + 1)
                wait(e, "mm_taken", n - 1)
                for k, t in enumerate(ts):
                    last = e.matmul(om[u][:, k * m:(k + 1) * m], hT[0:kd, u, k * P:(k + 1) * P],
                                    rhs, start=True, stop=True)
                last.then_inc(sem("mm_done"), 1)

        def mm_scalar(e, name, g, kd):
            for n, u, ts in batches(name, g):
                wait(e, "mm_turned", n + 1)
                wait(e, "mm_done", n - 1)
                e.activation(hT[0:kd, u, 0:len(ts) * P], tp[u][0:kd, 0:len(ts) * P], ACT.Copy)\
                    .then_inc(sem("mm_copied"), 1)

        def mm_vector(e, name, g, m, take):
            for n, u, ts in batches(name, g):
                wait(e, "mm_done", n + 1)
                take(om[u][:, 0:len(ts) * m].rearrange("p (n m) -> p n m", n=len(ts)), ts[0], len(ts))\
                    .then_inc(sem("mm_taken"), 1)
            e.wait_ge(sem("mm_taken"), n + 1)

        def norm_vector(e, chain, g):
            ts = slice(g * NT, (g + 1) * NT)
            xs, h, m = X[:, ts, :], H[:, ts, :], M[:, ts, :]
            mean, var = stat["mean"][:, ts], stat["var"][:, ts]
            chain(e.tensor_reduce(out=mean, in_=xs, op=ALU.add, axis=AX.X))
            chain(e.tensor_scalar(mean, mean, 1.0 / D, None, ALU.mult))
            chain(e.tensor_tensor(h, xs, bcast(mean), ALU.subtract))
            chain(e.tensor_tensor(m, h, h, ALU.mult))
            e.tensor_reduce(out=var, in_=m, op=ALU.add, axis=AX.X).then_inc(sem("var"), 1)

        def norm_rest(e, chain, l, g):
            ts = slice(g * NT, (g + 1) * NT)
            h, rstd = H[:, ts, :], stat["rstd"][:, ts]
            e.wait_ge(sem("std"), l * NGROUPS + g + 1)
            chain(e.reciprocal(rstd, rstd))
            chain(e.scalar_tensor_tensor(out=h, in0=h, scalar=0.0, in1=bcast(rstd), op0=ALU.max, op1=ALU.mult))

        def norm_scalar(e, l, g):
            ts = slice(g * NT, (g + 1) * NT)
            e.wait_ge(sem("var"), l * NGROUPS + g + 1)
            e.activation(stat["rstd"][:, ts], stat["var"][:, ts], ACT.Sqrt, bias=eps[:, 0:1], scale=1.0 / D)\
                .then_inc(sem("std"), 1)

        def divide_steps(e, val, n):
            q, r, t, ti = hq[:, 0:n], hr[:, 0:n], ht[:, 0:n], hi[:, 0:n]
            yield e.tensor_scalar(ti, val, 1.0 / TILES, None, ALU.mult)
            yield e.tensor_copy(q, ti)
            yield e.scalar_tensor_tensor(out=r, in0=q, scalar=-float(TILES), in1=val, op0=ALU.mult, op1=ALU.add)
            yield e.tensor_scalar(t, r, 0.0, None, ALU.is_lt)
            yield e.tensor_tensor(q, q, t, ALU.subtract)
            yield e.scalar_tensor_tensor(out=r, in0=t, scalar=float(TILES), in1=r, op0=ALU.mult, op1=ALU.add)
            yield e.tensor_scalar(t, r, float(TILES), None, ALU.is_ge)
            yield e.tensor_tensor(q, q, t, ALU.add)
            yield e.scalar_tensor_tensor(out=r, in0=t, scalar=-float(TILES), in1=r, op0=ALU.mult, op1=ALU.add)

        def divide(e, chain, val, n):
            for ins in divide_steps(e, val, n):
                chain(ins)

        def onehot_steps(e, name, base, groups):
            for g in groups:
                k = g % HBUF
                wait(e, name + "_used", base + g - HBUF + 1)
                for c in range(HG):
                    j = g * HG + c
                    yield e.tensor_scalar(oh_q[:, k, c, :], iota_b[:, :], hq[:, j:j + 1], None, ALU.is_equal)
                    last = e.tensor_scalar(oh_r[:, k, c, :], iota_b[:, 0:TILES], hr[:, j:j + 1], None, ALU.is_equal)
                    if c == HG - 1:
                        last.then_inc(sem(name + "_made"), 1)
                    yield last

        def onehots(e, name, base, groups):
            for _ in onehot_steps(e, name, base, groups):
                pass

        def block_numbers(e, b, r):
            side = Chain(e, "v_side")
            for k, ins in enumerate(divide_numbers(e, r)):
                side.n += 1
                ins.then_inc(sem("v_side"), 1)
                yield
                e.wait_ge(sem("v_side"), side.n)
            side.clear()
            yield from onehot_steps(e, "hs", b * (K // HG), [0])

        def divide_numbers(e, r):
            yield e.tensor_copy(srcf[:, :], idx[:, r, :])
            yield from divide_steps(e, srcf[:, :], K)

        def count_tensor(e, name, base, groups, first):
            for g in range(groups):
                k = g % HBUF
                wait(e, name + "_made", base + g + 1)
                for c in range(HG):
                    last = e.matmul(hist[:, :], oh_q[:, k, c, :], oh_r[:, k, c, :],
                                    start=first and g == 0 and c == 0, stop=c == HG - 1,
                                    skip_group_check=True)
                last.then_inc(sem(name + "_used"), 1)

        PGRP = PIVOTS // HG

        raw_src = ring[:, :, :, :].rearrange("p r k f -> p (r k f)")[:, 0:LANE].bitcast(i32)
        raw_w = ring[:, :, :, :].rearrange("p r k f -> p (r k f)")[:, LANE:2 * LANE]
        raw_dst = keep[:, :].bitcast(i32)
        SGRP = PIVOTS // HG
        SITERS = LANE // PIVOTS

        def unsorted(e):
            e.wait_ge(sem("judged"), 1)
            return e.If(e.value_load(bad_i[0:1, 0:1], min_val=0, max_val=2 * E) > 0)

        def each_column(e, body):
            body(0)
            with e.Fori(1, LANE) as c:
                body(c)

        def sort_vector(e):
            ch = Chain(e, "v_loop")

            def count(i):
                divide(e, ch, dst_f[:, bass.ds(i * PIVOTS, PIVOTS)], PIVOTS)
                onehots(e, "hg", i * SGRP, range(SGRP))
                wait(e, "hg_made", i * SGRP + SGRP)
                gate(e)
                ch.clear()
            count(0)
            with e.Fori(1, SITERS) as i:
                count(i)
            e.wait_ge(sem("hg_used"), LANE // HG)
            ch(e.tensor_copy(stat["deg"][:, :], hist[:, :]))
            ch(e.tensor_tensor_scan(out=stat["incl"][:, :], data0=ones[:, :], data1=stat["deg"][:, :],
                                    initial=0.0, op0=ALU.mult, op1=ALU.add))
            ch(e.tensor_copy(col["tot"][:, :], stat["incl"][:, TILES - 1:TILES]))
            e.sem_inc(sem("g_counted"), 1)
            e.wait_ge(sem("g_offset"), 1)
            ch(e.tensor_copy(col["offs"][:, :], pa[:, 0:1]))
            ch(e.tensor_tensor(stat["incl"][:, :], stat["incl"][:, :], stat["deg"][:, :], ALU.subtract))
            ch(e.tensor_scalar(stat["tmp"][:, :], stat["incl"][:, :], col["offs"][:, 0:1], None, ALU.add))
            ch.clear()
            e.sem_inc(sem("g_table"), 1)
            e.wait_ge(sem("g_raw"), 32)

            def column(c):
                wait(e, "g_settled", c)
                gate(e)
                ch(e.tensor_copy(c_dst[:, :], raw_dst[:, bass.ds(c, 1)]))
                ch(e.tensor_copy(c_src[:, :], raw_src[:, bass.ds(c, 1)]))
                ch(e.tensor_copy(c_w[:, :], raw_w[:, bass.ds(c, 1)]))
                ch(e.tensor_copy(c_dst_f[:, :], c_dst[:, :]))
                e.sem_inc(sem("g_column"), 1)
                wait(e, "g_spread", c + 1)
                gate(e)
                ch(e.scalar_tensor_tensor(out=match[:, 0, :], in0=pa[:, :], scalar=c_dst_f[:, 0:1],
                                          in1=earlier[:, :], op0=ALU.is_equal, op1=ALU.mult,
                                          accum_out=c_rank[:, :]))
                ch(e.scalar_tensor_tensor(out=match[:, 1, :], in0=pa[:, :], scalar=c_dst_f[:, 0:1],
                                          in1=before[:, :], op0=ALU.is_equal, op1=ALU.mult,
                                          accum_out=c_after[:, :]))
                ch(e.tensor_scalar(c_after[:, :], c_after[:, :], 0.0, None, ALU.is_gt))
                ch(e.tensor_tensor(c_step[:, :], spare[:, :], c_dst_f[:, :], ALU.subtract))
                ch(e.tensor_tensor(c_step[:, :], c_step[:, :], c_after[:, :], ALU.mult))
                ch(e.tensor_tensor(c_home[:, :], c_step[:, :], c_dst_f[:, :], ALU.add))
                wait(e, "g_next", c * 16 + 16)
                gate(e)
                ch(e.tensor_tensor(c_pos[:, :], c_next[:, :], c_rank[:, :], ALU.add))
                ch(e.scalar_tensor_tensor(out=c_new[:, :], in0=c_next[:, :], scalar=1.0, in1=c_rank[:, :],
                                          op0=ALU.add, op1=ALU.add))
                ch.clear()
                e.sem_inc(sem("g_placed"), 1)
            each_column(e, column)
            e.wait_ge(sem("g_back"), 32)
            lane_tables(e, ch)
            ch.clear()

        def sort_tensor(e):
            count_tensor(e, "hg", 0, SGRP, True)
            with e.Fori(1, SITERS) as i:
                count_tensor(e, "hg", i * SGRP, SGRP, False)
            e.wait_ge(sem("g_counted"), 1)
            e.matmul(pa[:, 0:1], before[:, :], col["tot"][:, :], start=True, stop=True)\
                .then_inc(sem("g_offset"), 1)

            def column(c):
                wait(e, "g_column", c + 1)
                gate(e)
                e.matmul(pa[:, :], c_dst_f[:, 0:1].broadcast_to([P, P]), ident[:, :], start=True, stop=True)\
                    .then_inc(sem("g_spread"), 1)
            each_column(e, column)

        def sort_gpsimd(e):
            e.dma_start(raw_src, lanes(src)).then_inc(sem("g_raw"), 16)
            e.dma_start(raw_w, lanes(edge_weight)).then_inc(sem("g_raw"), 16)
            e.wait_ge(sem("g_table"), 1)
            e.dma_start(places[0:ROWS, :].rearrange("(p t) o -> p (t o)", p=P), stat["tmp"][:, :])\
                .then_inc(sem("g_ready"), 16)
            e.dma_start(places[ROWS:ROWS + P, :], zero_row[:, 0:1]).then_inc(sem("g_ready"), 16)
            e.wait_ge(sem("g_ready"), 32)

            def column(c):
                wait(e, "g_column", c + 1)
                gate(e)
                e.indirect_dma_start(out=c_next[:, :], out_offset=None, in_=places[:, :],
                                     in_offset=bass.IndirectOffsetOnAxis(ap=c_dst[:, 0:1], axis=0))\
                    .then_inc(sem("g_next"), 16)
                wait(e, "g_placed", c + 1)
                gate(e)
                for put, table, where, value in (("g_put_dst", e_dst, c_pos, c_dst),
                                                 ("g_put_src", e_src, c_pos, c_src),
                                                 ("g_put_w", e_weight, c_pos, c_w),
                                                 ("g_put_next", places, c_home, c_new)):
                    e.indirect_dma_start(out=table[:, :],
                                         out_offset=bass.IndirectOffsetOnAxis(ap=where[:, 0:1], axis=0),
                                         in_=value[:, :], in_offset=None).then_inc(sem(put), 16)
                for put in ("g_put_dst", "g_put_src", "g_put_w", "g_put_next"):
                    wait(e, put, c * 16 + 16)
                    gate(e)
                e.sem_inc(sem("g_settled"), 1)
            each_column(e, column)
            e.dma_start(raw_dst, dst_l).then_inc(sem("g_back"), 16)
            e.dma_start(prev_i[1:P, :], dst_l[0:P - 1, LANE - 1:LANE], allow_slow_non_contiguous=True)\
                .then_inc(sem("g_back"), 16)
            e.wait_ge(sem("g_back"), 32)

        def lane_tables(e, ch):
            ch(e.tensor_copy(first_i[:, :], raw_dst[:, 0:1]))
            ch(e.tensor_copy(dst_f[:, :], raw_dst))
            ch(e.tensor_copy(col["first"][:, :], first_i[:, :]))
            ch(e.tensor_copy(col["prev"][:, :], prev_i[:, :]))

        def gather_slot(e, l, i, r, table):
            wait(e, f"indexed{r}", i * 16 + (l * 16 * ITERS + 16))
            gate(e)
            for j in range(K):
                e.indirect_dma_start(out=ring[:, r, j, :], out_offset=None, in_=table[:, :],
                                     in_offset=bass.IndirectOffsetOnAxis(ap=idx[:, r, j:j + 1], axis=0))\
                    .then_inc(sem(f"gathered{l}_{r}"), 16)

        def pass_index(e, l, i, r):
            wait(e, f"gathered{l}_{r}", i * (16 * K))
            gate(e)
            wait(e, "scanned", l * BLOCKS if isinstance(i, int) else i * R + (l * BLOCKS + r - R + 2))
            gate(e)
            wait(e, f"stored{r}", i * 16 + l * 16 * ITERS)
            gate(e)
            e.dma_start(idx[:, r, :], src_l[:, bass.ds((i * R + r) * K, K)]).then_inc(sem(f"indexed{r}"), 16)

        def pass_store(e, l, i, r):
            wait(e, "scanned", i * R + (l * BLOCKS + r + 1))
            e.dma_start(lrows(edge_rows)[:, bass.ds((i * R + r) * K, K), :], ring[:, r, :, :])\
                .then_inc(sem(f"stored{r}"), 16)

        def load_masks(e, chain, i, r):
            chain(e.tensor_copy(mblk[:, 0, :], keep[:, bass.ds((i * R + r) * K, K)]))

        def scan_columns(e, chain, buf, b, r, mask, op0, op1, cols, other=None, meanwhile=iter(())):
            for n, j in enumerate(cols):
                prev = buf[:, r, j - 1, :] if j else buf[:, (r - 1) % R, K - 1, :]
                if isinstance(b, int) and b + j == 0:
                    prev = zero_row[:, :]
                this = buf[:, r, j, :] if other is None else other[:, n * D:(n + 1) * D]
                chain(e.scalar_tensor_tensor(out=buf[:, r, j, :], in0=prev, scalar=mask[:, j:j + 1],
                                             in1=this, op0=op0, op1=op1), meanwhile)

        def sum_pass_vector(e, l):
            chain = Chain(e, "v_loop")
            chain(e.memset(M, 0.0))
            if l == 2:
                chain(e.memset(fill[:, :, :, :], 0.0))
                e.sem_inc(sem("fill_clear"), 1)
            chain.clear()
            e.sem_inc(sem("cleared"), 1)

            def body(i):
                for r in range(R):
                    load_masks(e, chain, i, r)
                    wait(e, f"gathered{l}_{r}", i * (16 * K) + 16 * K)
                    scan_columns(e, chain, ring, i * R + r, r, mblk[:, 0, :], ALU.mult, ALU.add, range(K))
                    chain.clear()
                    e.sem_inc(sem("scanned"), 1)
            loop(e, body)

        def fix_tensor(e, l):
            e.wait_ge(sem("tailed"), l + 1)
            e.transpose(pa[0:D, 0:P], tail[:, :], ident[:, :]).then_inc(sem("tail_turned"), 1)
            e.wait_ge(sem("carried"), l + 1)
            e.transpose(pb[:, 0:D], carryT[:, 0:P], ident[0:D, 0:D]).then_inc(sem("carry_turned"), 1)

        def fix_vector(e, chain, l, op0, op1, row, colc):
            e.tensor_copy(tail[:, :], ring[:, R - 1, K - 1, :]).then_inc(sem("tailed"), 1)
            e.wait_ge(sem("tail_turned"), l + 1)
            e.tensor_tensor_scan(out=carryT[:, 1:P + 1], data0=row[:, :], data1=pa[0:D, 0:P], initial=0.0,
                                 op0=op0, op1=op1).then_inc(sem("carried"), 1)
            e.wait_ge(sem("carry_turned"), l + 1)
            e.wait_ge(sem("fix_read"), 16 * (l + 1))
            e.scalar_tensor_tensor(out=fixrow[:, :], in0=pb[:, 0:D], scalar=colc[:, 0:1], in1=fixrow[:, :],
                                   op0=op0, op1=op1).then_inc(sem("fix_made"), 1)

        def fix_gpsimd(e, l):
            for r in range(R):
                e.wait_ge(sem(f"stored{r}"), 16 * ITERS * (l + 1))
            e.indirect_dma_start(out=fixrow[:, :], out_offset=None, in_=edge_rows[:, :],
                                 in_offset=bass.IndirectOffsetOnAxis(ap=fix_i[:, 0:1], axis=0))\
                .then_inc(sem("fix_read"), 16)
            e.wait_ge(sem("fix_made"), l + 1)
            e.indirect_dma_start(out=edge_rows[:, :], out_offset=bass.IndirectOffsetOnAxis(ap=fix_i[:, 0:1], axis=0),
                                 in_=fixrow[:, :], in_offset=None).then_inc(sem("fix_written"), 16)
            e.wait_ge(sem("fix_written"), 16 * (l + 1))
            e.wait_ge(sem("cleared"), l + 1)
            for t in range(TILES):
                e.indirect_dma_start(out=M[:, t, :], out_offset=None, in_=edge_rows[:, :],
                                     in_offset=bass.IndirectOffsetOnAxis(ap=end_i[:, t:t + 1], axis=0),
                                     bounds_check=E - 1, oob_is_err=False).then_inc(sem(f"node_rows{t // NT}"), 16)

        def first_rows_gpsimd(e, k, table):
            for t in range(TILES):
                e.indirect_dma_start(out=first_rows[:, :],
                                     out_offset=bass.IndirectOffsetOnAxis(ap=start_i[:, t:t + 1], axis=0),
                                     in_=H[:, t, :], in_offset=None,
                                     bounds_check=E - 1, oob_is_err=False).then_inc(sem(f"placed{k}"), 16)
            e.indirect_dma_start(out=lane_init[:, :], out_offset=None, in_=table[:, :],
                                 in_offset=bass.IndirectOffsetOnAxis(ap=first_i[:, 0:1], axis=0))\
                .then_inc(sem(f"lane_read{k}"), 16)

        def lane_start_sync(e, k):
            e.wait_ge(sem(f"placed{k}"), 16 * TILES)
            e.wait_ge(sem(f"lane_read{k}"), 16)
            e.dma_start(lrows(first_rows)[:, 0, :], lane_init[:, :]).then_inc(sem(f"lane_placed{k}"), 16)
            e.wait_ge(sem(f"lane_placed{k}"), 16)

        def load_fill(e, l, i, r):
            if not isinstance(i, int):
                wait(e, f"filled{l}", i * R + (r - R + 2))
                gate(e)
            e.dma_start(fill[:, r, :, :], lrows(first_rows)[:, bass.ds((i * R + r) * K, K), :])\
                .then_inc(sem(f"first{l}_{r}"), 16)

        MAXQ = [list(range(a, min(a + 8, K))) for a in range(0, K, 8)]
        NQ = len(MAXQ)
        assert NQ % 2 == 0

        def pairs(cols):
            return [cols[a:a + 2] for a in range(0, len(cols), 2)]

        LASTQ = [list(range(a, min(a + 4, K))) for a in range(0, K, 4)]
        NL = len(LASTQ)

        def back(q):
            return next(m for m in range(1, NL + 1) if (q - m if q >= m else q - m + NL) % 2 == q % 2)

        GROUPS = R * K // ACC_PER_SET
        SET_GROUPS = [len(range(s, GROUPS, ACC_SETS)) for s in range(ACC_SETS)]

        def wait_slot_added(e, i, r):
            if not (isinstance(i, int) and i == 0):
                for s in range(ACC_SETS):
                    upto = len(range(s, (r + 1) * K // ACC_PER_SET, ACC_SETS))
                    wait(e, f"added{s}", i * (16 * ACC_PER_SET * SET_GROUPS[s])
                         - 16 * ACC_PER_SET * (SET_GROUPS[s] - upto))

        def acc_buf(g, k):
            t = (ring if g % 2 else fill)[:, :, :, :].rearrange("p r k f -> p (r k) f")
            return t[:, k * NT:(k + 1) * NT, :]

        block = ctx.enter_context(nc.Block())

        def store_table(e, l, table):
            for g in range(NGROUPS):
                ts = slice(g * NT, (g + 1) * NT)
                e.wait_ge(sem("table_made"), (l - 1) * NGROUPS + g + 1)
                e.dma_start(nrows(table)[:, ts, :], H[:, ts, :]).then_inc(sem(f"tab{l}"), 16)

        @block.sync
        def _(e):
            e.dma_start(raw_dst, lanes(dst)).then_inc(sem("dst_in"), 16)
            e.wait_ge(sem("const"), 1)
            e.dma_start(prev_i[1:P, :], lanes(dst)[0:P - 1, LANE - 1:LANE], allow_slow_non_contiguous=True)\
                .then_inc(sem("dst_in"), 16)
            for to, of in ((e_dst, dst), (e_src, src), (e_weight, edge_weight)):
                e.dma_start(lanes1(to), lanes(of)).then_inc(sem("copied"), 16)
            e.wait_ge(sem("x_padded"), 1)
            e.dma_start(X[0:P - 1, :, :], x[0:(P - 1) * TILES, :].rearrange("(p t) f -> p t f", t=TILES))\
                .then_inc(sem("x_in"), 16)
            e.dma_start(X[P - 1:P, 0:LAST_ROWS, :], x[(P - 1) * TILES:N, :].rearrange("(p t) f -> p t f", p=1))\
                .then_inc(sem("x_in"), 16)
            for tile, w in ((w_ab[:, 0:D], l0_w1[0:D, :]), (w_ab[:, D:2 * D], l0_w1[D:2 * D, :]),
                            (w_gcn[:, :], l1_w[:, :]), (w_hop1[:, :], l2_w1[:, :]), (w_hop2[:, :], l2_w2[:, :]),
                            (w_lastT[:, 0:D], l3_ws[:, :]), (w_lastT[:, D:2 * D], l3_wn[:, :]),
                            *((bias[n][:, :], brow(b)) for n, b in (
                                ("e1", l0_b1), ("e2", l0_b2), ("gcn", l1_b), ("hop1", l2_b1), ("hop2", l2_b2),
                                ("last", l3_bs), ("last2", l3_bn)))):
                e.dma_start(tile, w).then_inc(sem("w_in"), 16)
            e.wait_ge(sem("diag_clear"), 1)
            e.dma_start(w_diag[0:D, 0:D], l0_w2[:, :]).then_inc(sem("w_in"), 16)
            e.dma_start(w_diag[D:P, D:P], l0_w2[:, :]).then_inc(sem("w_in"), 16)
            e.wait_ge(sem("ordered"), 1)
            for r in range(R):
                pass_index(e, 0, 0, r)
            for g in range(NGROUPS):
                ts = slice(g * NT, (g + 1) * NT)
                e.wait_ge(sem("ab_made"), g + 1)
                e.dma_start(nrows(tab_edge_b)[:, ts, :], M[:, ts, :]).then_inc(sem("tab0"), 16)
            e.dma_start(nrows(tab_edge_a), H).then_inc(sem("tab_a"), 16)
            lane_start_sync(e, 0)
            for r in range(R):
                load_fill(e, 0, 0, r)
            with e.Fori(1, ITERS) as i:
                for r in range(R):
                    pass_index(e, 0, i, r)
                    load_fill(e, 0, i, r)
            for l, table in ((1, tab_gcn), (2, tab_hop1), (3, tab_hop2)):
                store_table(e, l, table)

                def body(i):
                    for r in range(R):
                        pass_index(e, l, i, r)
                loop(e, body)
                if l == 2:
                    e.wait_ge(sem("fill_clear"), 2)
                    for a in accs:
                        e.dma_start(a.rearrange("(p t) f -> p t f", p=P),
                                    fill[:, :, :, :].rearrange("p r k f -> p (r k) f")[:, 0:TILES + 1, :])\
                            .then_inc(sem("acc_zeroed"), 16)
            e.wait_ge(sem("acc_zeroed"), 16 * len(accs))
            store_table(e, 4, tab_last)
            lane_start_sync(e, 1)

            def body4(i):
                for r in range(R):
                    wait(e, "messages", (i * R + (r - R + 1)) * NL)
                    gate(e)
                    load_fill(e, 4, i, r)
                    e.dma_start(idx[:, r, :], src_l[:, bass.ds((i * R + r) * K, K)]).then_inc(sem(f"first4_{r}"), 16)
                    e.dma_start(wblk[:, r, :], w_l[:, bass.ds((i * R + r) * K, K)]).then_inc(sem(f"first4_{r}"), 16)
            loop(e, body4)
            for s in range(ACC_SETS):
                e.wait_ge(sem(f"added{s}"), 16 * ACC_PER_SET * SET_GROUPS[s] * ITERS)
            for g in range(NGROUPS):
                ts = slice(g * NT, (g + 1) * NT)
                wait(e, "aggregated", 3 * NGROUPS + g - 1)
                for k, a in enumerate(accs):
                    e.dma_start(acc_buf(g, k), nrows(a[0:ROWS, :])[:, ts, :]).then_inc(sem(f"acc_in{g % 2}"), 16)
            e.wait_ge(sem("x_final"), 1)
            e.dma_start(out[0:(P - 1) * TILES, :].rearrange("(p t) f -> p t f", t=TILES), X[0:P - 1, :, :])\
                .then_inc(sem("x_out"), 16)
            e.dma_start(out[(P - 1) * TILES:N, :].rearrange("(p t) f -> p t f", p=1), X[P - 1:P, 0:LAST_ROWS, :])\
                .then_inc(sem("x_out"), 16)
            e.wait_ge(sem("x_out"), 32)

        @block.gpsimd
        def _(e):
            chain = Chain(e, "g_chain")
            chain(e.memset(ident[:, :], 0.0))
            chain(e.memset(before[:, :], 1.0))
            chain(e.memset(earlier[:, :], 1.0))
            chain(e.affine_select(out=ident[:, :], in_=ident[:, :], compare_op=ALU.not_equal, fill=1.0,
                                  base=0, pattern=[[-1, P]], channel_multiplier=1))
            chain(e.affine_select(out=before[:, :], in_=before[:, :], compare_op=ALU.is_gt, fill=0.0,
                                  base=0, pattern=[[1, P]], channel_multiplier=-1))
            chain(e.affine_select(out=earlier[:, :], in_=earlier[:, :], compare_op=ALU.is_gt, fill=0.0,
                                  base=0, pattern=[[-1, P]], channel_multiplier=1))
            chain(e.iota(iota_i[:, :], pattern=[[1, P]], base=0, channel_multiplier=0))
            chain(e.iota(colp_i[:, 0:1], pattern=[[0, 1]], base=0, channel_multiplier=LANE))
            chain(e.iota(colp_i[:, 1:2], pattern=[[0, 1]], base=ROWS, channel_multiplier=1))
            chain(e.memset(prev_i[:, :], -1))
            chain(e.iota(node_i[:, :], pattern=[[1, TILES + 1]], base=0, channel_multiplier=TILES))
            e.sem_inc(sem("const"), 1)
            e.wait_ge(sem("copied"), 48)
            with unsorted(e):
                sort_gpsimd(e)
            e.sem_inc(sem("ordered"), 1)
            e.wait_ge(sem("chunked"), 1)
            for t in range(TILES + 1):
                e.indirect_dma_start(out=chunks[:, t, 0:CHUNK].bitcast(i32), out_offset=None,
                                     in_=e_dst.rearrange("(c k) o -> c (k o)", k=CHUNK),
                                     in_offset=bass.IndirectOffsetOnAxis(ap=chunk_i[:, t:t + 1], axis=0))\
                    .then_inc(sem("chunks_in"), 16)
            e.wait_ge(sem("tab0"), 16 * NGROUPS)
            e.wait_ge(sem("placeable"), 1)
            for r in range(AHEAD):
                gather_slot(e, 0, 0, r, tab_edge_b)
            e.wait_ge(sem("tab_a"), 16)
            e.wait_ge(sem("zeroed"), 16 * (LANE // (R * K)))
            first_rows_gpsimd(e, 0, tab_edge_a)
            for r in range(AHEAD, R):
                gather_slot(e, 0, 0, r, tab_edge_b)
            with e.Fori(1, ITERS) as i:
                for r in range(R):
                    gather_slot(e, 0, i, r, tab_edge_b)
            fix_gpsimd(e, 0)
            for l, table in ((1, tab_gcn), (2, tab_hop1), (3, tab_hop2)):
                e.wait_ge(sem(f"tab{l}"), 16 * NGROUPS)

                def body(i):
                    for r in range(R):
                        gather_slot(e, l, i, r, table)
                loop(e, body)
                fix_gpsimd(e, l)
            e.wait_ge(sem("tab4"), 16 * NGROUPS)
            first_rows_gpsimd(e, 1, tab_last)
            e.wait_ge(sem("acc_zeroed"), 16 * len(accs))

            def body4(i):
                for r in range(R):
                    wait(e, "messages", (i * R + r) * NL + NL)
                    wait(e, "targets", i * R + (r + 1))
                    gate(e)
                    for g in range(K // ACC_PER_SET):
                        G = r * (K // ACC_PER_SET) + g
                        s = G % ACC_SETS
                        n = i * SET_GROUPS[s] + G // ACC_SETS
                        if not (isinstance(n, int) and n == 0):
                            wait(e, f"added{s}", n * (16 * ACC_PER_SET))
                            gate(e)
                        for a in range(ACC_PER_SET):
                            j = g * ACC_PER_SET + a
                            e.indirect_dma_start(
                                out=accs[s * ACC_PER_SET + a][:, :],
                                out_offset=bass.IndirectOffsetOnAxis(ap=idx2[:, r, j:j + 1], axis=0),
                                in_=ring[:, r, j, :], in_offset=None, compute_op=ALU.add)\
                                .then_inc(sem(f"added{s}"), 16)
            loop(e, body4)

        @block.vector
        def _(e):
            chain = Chain(e, "v_chain")
            e.memset(fill[:, :, :, :], 0.0).then_inc(sem("fill_clear"), 1)
            e.memset(X[96:P, :, :], 0.0).then_inc(sem("x_padded"), 1)
            e.memset(w_diag[:, :], 0.0).then_inc(sem("diag_clear"), 1)
            chain(e.memset(zero_row[:, :], 0.0))
            e.wait_ge(sem("const"), 1)
            chain(e.tensor_copy(iota_b[:, :], iota_i[:, :]))
            chain(e.tensor_copy(lane0[:, :], colp_i[:, 0:1]))
            chain(e.tensor_copy(spare[:, :], colp_i[:, 1:2]))
            chain(e.memset(ones[:, :], 1.0))
            chain(e.memset(carryT[:, :], 0.0))
            chain(e.memset(eps[:, :], 1e-5))
            chain(e.tensor_copy(node_f[:, :], node_i[:, :]))
            e.wait_ge(sem("dst_in"), 32)
            lane_tables(e, chain)
            chain(e.scalar_tensor_tensor(out=oh_flat[:, 1:LANE], in0=dst_f[:, 1:LANE], scalar=0.0,
                                         in1=dst_f[:, 0:LANE - 1], op0=ALU.add, op1=ALU.is_lt,
                                         accum_out=bad[:, 0:1]))
            chain(e.tensor_tensor(bad[:, 1:2], col["first"][:, :], col["prev"][:, :], ALU.is_lt))
            e.sem_inc(sem("checked"), 1)
            e.wait_ge(sem("bad_counted"), 1)
            chain(e.tensor_copy(bad_i[0:1, 0:1], pb[0:1, 0:1]))
            e.sem_inc(sem("judged"), 1)
            with unsorted(e):
                sort_vector(e)
            chain(e.tensor_tensor(keep[:, 1:LANE], dst_f[:, 1:LANE], dst_f[:, 0:LANE - 1], ALU.is_equal))
            chain(e.memset(keep[:, 0:1], 0.0))
            loop_chain = Chain(e, "v_loop")
            chain(e.tensor_copy(pivot[:, :], dst_f[:, 0:LANE:CHUNK]))
            divide(e, chain, pivot[:, :], PIVOTS)
            onehots(e, "hd", 0, range(PGRP))
            e.wait_ge(sem("hd_used"), PGRP)
            chain(e.tensor_scalar(oh_flat[:, 0:LANE], dst_f[:, :], col["first"][:, 0:1], 0.0, ALU.is_equal, ALU.add,
                                  accum_out=col["cnt"][:, :]))
            chain(e.tensor_scalar(limit[:, :], keep[:, :], 2.0, -1.0, ALU.mult, ALU.add))
            chain(e.tensor_scalar(limit[:, :], limit[:, :], FULL, None, ALU.mult))
            chain(e.scalar_tensor_tensor(out=fix_i[:, :], in0=col["cnt"][:, :], scalar=-1.0, in1=lane0[:, :],
                                         op0=ALU.add, op1=ALU.add))
            chain(e.tensor_tensor(col["cont"][:, :], col["first"][:, :], col["prev"][:, :], ALU.is_equal))
            chain(e.tensor_scalar(col["whole"][:, :], col["cnt"][:, :], float(LANE), None, ALU.is_equal))
            chain(e.tensor_tensor(col["k"][:, :], col["whole"][:, :], col["cont"][:, :], ALU.mult))
            chain(e.tensor_scalar(col["contL"][:, :], col["cont"][:, :], 2.0, -1.0, ALU.mult, ALU.add))
            chain(e.tensor_scalar(col["contL"][:, :], col["contL"][:, :], FULL, None, ALU.mult))
            chain(e.tensor_tensor_scan(out=stat["incl"][:, :], data0=ones[:, :], data1=hist[:, :],
                                       initial=0.0, op0=ALU.mult, op1=ALU.add))
            chain(e.tensor_copy(col["tot"][:, :], stat["incl"][:, TILES - 1:TILES]))
            e.sem_inc(sem("counted"), 1)
            e.wait_ge(sem("offset"), 1)
            chain(e.tensor_copy(col["offs"][:, :], pa[:, 0:1]))
            chain(e.tensor_copy(krow[:, :], pb[0:D, :]))
            chain(e.tensor_scalar(krowL[:, :], krow[:, :], 2.0, -1.0, ALU.mult, ALU.add))
            chain(e.tensor_scalar(krowL[:, :], krowL[:, :], FULL, None, ALU.mult))
            chain(e.tensor_copy(chunk_f[:, 0:1], col["offs"][:, :]))
            chain(e.tensor_scalar(chunk_f[:, 1:TILES + 1], stat["incl"][:, :], col["offs"][:, 0:1], None, ALU.add))
            chain(e.tensor_scalar(chunk_f[:, :], chunk_f[:, :], -1.0, 0.0, ALU.add, ALU.max))
            chain(e.tensor_copy(chunk_i[:, :], chunk_f[:, :]))
            e.sem_inc(sem("chunked"), 1)

            def take_ab(p, t, n):
                e.tensor_tensor(H[:, t:t + n, :], p[:, :, 0:D], brow3(bias["e1"][:, :], n), ALU.add)
                return e.tensor_copy(M[:, t:t + n, :], p[:, :, D:2 * D])

            def place_nodes():
                e.wait_ge(sem("chunks_in"), 16 * (TILES + 1))
                mc = chunks[:, 0:TILES + 1, 0:CHUNK]
                chain(e.tensor_tensor(mc, mc.bitcast(i32), bcast(node_f[:, :], CHUNK), ALU.is_lt))
                chain(e.tensor_reduce(out=edge0[:, :], in_=mc, op=ALU.add, axis=AX.X))
                chain(e.scalar_tensor_tensor(out=edge0[:, :], in0=chunk_f[:, :], scalar=float(CHUNK), in1=edge0[:, :],
                                             op0=ALU.mult, op1=ALU.add))
                chain(e.tensor_tensor(stat["deg"][:, :], edge0[:, 1:TILES + 1], edge0[:, 0:TILES], ALU.subtract))
                chain(e.tensor_scalar(stat["has"][:, :], stat["deg"][:, :], 0.0, None, ALU.is_gt))
                chain(e.tensor_scalar(stat["tmp"][:, :], stat["has"][:, :], -BEYOND, BEYOND, ALU.mult, ALU.add))
                chain(e.tensor_tensor(start_i[:, :], stat["tmp"][:, :], edge0[:, 0:TILES], ALU.add))
                chain(e.scalar_tensor_tensor(out=end_i[:, :], in0=stat["tmp"][:, :], scalar=-1.0,
                                             in1=edge0[:, 1:TILES + 1], op0=ALU.add, op1=ALU.add))
                e.sem_inc(sem("placeable"), 1)
                chain(e.tensor_scalar(stat["deg"][:, :], stat["deg"][:, :], 1.0, None, ALU.max))
                chain(e.reciprocal(stat["inv"][:, :], stat["deg"][:, :]))
                e.sem_inc(sem("degrees"), 1)

            e.wait_ge(sem("w_in"), 16 * 16)
            chain(e.tensor_tensor(w_ab[:, 0:D], w_ab[:, 0:D], w_ab[:, D:2 * D], ALU.subtract))
            chain(e.tensor_tensor(bias["last"][:, :], bias["last"][:, :], bias["last2"][:, :], ALU.add))
            e.wait_ge(sem("x_in"), 32)
            for g in range(NGROUPS + 2):
                if g < NGROUPS:
                    norm_vector(e, chain, g)
                if g == NGROUPS - 2:
                    place_nodes()
                if g and g - 1 < NGROUPS:
                    norm_rest(e, chain, 0, g - 1)
                    e.sem_inc(sem("normed"), 1)
                if g > 1:
                    mm_vector(e, "ab", g - 2, 2 * D, take_ab)
                    e.sem_inc(sem("ab_made"), 1)

            SHOWN = range(1, 3)

            def body0(i):
                for r in range(R):
                    b = i * R + r
                    load_masks(e, loop_chain, i, r)
                    loop_chain(e.tensor_copy(mblk[:, 1, :], limit[:, bass.ds(b * K, K)]))
                    wait(e, f"first0_{r}", i * 16 + 16)
                    wait(e, f"gathered0_{r}", i * (16 * K) + 16 * K)
                    numbers = block_numbers(e, b, r)
                    scan_columns(e, loop_chain, fill, b, r, mblk[:, 0, :], ALU.mult, ALU.add, range(K),
                                 meanwhile=numbers)
                    e.sem_inc(sem("filled0"), 1)
                    loop_chain(e.tensor_tensor(ring[:, r, :, :], ring[:, r, :, :], fill[:, r, :, :], ALU.add))
                    e.sem_inc(sem("summed0"), 1)
                    for _ in numbers:
                        pass
                    onehots(e, "hs", b * (K // HG), SHOWN)
                    rest = onehot_steps(e, "hs", b * (K // HG), range(SHOWN[-1] + 1, K // HG))
                    for q, cols in enumerate(MAXQ):
                        wait(e, "products0", b * NQ + (q + 1))
                        scan_columns(e, loop_chain, ring, b, r, mblk[:, 1, :], ALU.min, ALU.max, cols, om[q % 2],
                                     meanwhile=rest)
                        e.sem_inc(sem("taken0"), 1)
                    for _ in rest:
                        pass
                    loop_chain.clear()
                    e.sem_inc(sem("scanned"), 1)
            e.wait_ge(sem("tab0"), 16 * NGROUPS)
            chain(e.memset(M, 0.0))
            e.sem_inc(sem("cleared"), 1)
            loop(e, body0)
            fix_vector(e, chain, 0, ALU.min, ALU.max, krowL, col["contL"])
            e.wait_ge(sem("hs_used"), LANE // HG)
            chain(e.tensor_scalar(stat["nsrc"][:, :], hist[:, :], 1.0, None, ALU.max))
            e.sem_inc(sem("degrees"), 1)
            e.wait_ge(sem("rooted"), 2)
            chain(e.reciprocal(stat["nsrc"][:, :], stat["nsrc"][:, :]))
            chain(e.reciprocal(stat["ndst"][:, :], stat["ndst"][:, :]))

            def update0(g):
                ts = slice(g * NT, (g + 1) * NT)
                h, m, xs = H[:, ts, :], M[:, ts, :], X[:, ts, :]
                e.wait_ge(sem(f"node_rows{g}"), 16 * NT)
                chain(e.tensor_tensor(m, m, brow3(bias["e2"][:, :], NT), ALU.add))
                chain(e.tensor_tensor(h, m, m, ALU.subtract))
                chain(e.scalar_tensor_tensor(out=h.bitcast(i32), in0=h, scalar=0.0, in1=bcast(stat["has"][:, ts]),
                                             op0=ALU.is_equal, op1=ALU.mult))
                chain(e.tensor_tensor(m, m, xs, ALU.add))
                chain(e.copy_predicated(xs, h.bitcast(i32), m))
                norm_vector(e, chain, g)
            for g in range(NGROUPS + 1):
                if g < NGROUPS:
                    update0(g)
                if g:
                    norm_rest(e, chain, 1, g - 1)
                    ts = slice((g - 1) * NT, g * NT)
                    chain(e.tensor_tensor(H[:, ts, :], H[:, ts, :], bcast(stat["nsrc"][:, ts]), ALU.mult))
                    e.sem_inc(sem("table_made"), 1)
            sum_pass_vector(e, 1)

            def take_gcn(p, t, n):
                h, xs = H[:, t:t + n, :], X[:, t:t + n, :]
                chain(e.tensor_tensor(h, p, brow3(bias["gcn"][:, :], n), ALU.add))
                chain(e.scalar_tensor_tensor(out=h, in0=h, scalar=0.01, in1=h, op0=ALU.mult, op1=ALU.max))
                return e.tensor_tensor(xs, xs, h, ALU.add)

            def take_hop1(p, t, n):
                h = H[:, t:t + n, :]
                chain(e.tensor_tensor(h, p, brow3(bias["hop1"][:, :], n), ALU.add))
                return e.tensor_scalar(h, h, 0.0, None, ALU.max)

            def take_add(name):
                def take(p, t, n):
                    h, xs = H[:, t:t + n, :], X[:, t:t + n, :]
                    chain(e.tensor_tensor(h, p, brow3(bias[name][:, :], n), ALU.add))
                    return e.tensor_tensor(xs, xs, h, ALU.add)
                return take

            def nodes(l, name, factor, take, norm):
                fix_vector(e, chain, l, ALU.mult, ALU.add, krow, col["cont"])
                for g in range(NGROUPS + 2):
                    if g < NGROUPS:
                        ts = slice(g * NT, (g + 1) * NT)
                        e.wait_ge(sem(f"node_rows{g}"), 16 * NT * (l + 1))
                        chain(e.tensor_tensor(M[:, ts, :], M[:, ts, :], bcast(stat[factor][:, ts]), ALU.mult))
                        e.sem_inc(sem("aggregated"), 1)
                    if g and g - 1 < NGROUPS:
                        mm_vector(e, name, g - 1, D, take)
                        if norm is None:
                            e.sem_inc(sem("table_made"), 1)
                        else:
                            norm_vector(e, chain, g - 1)
                    if g > 1 and norm is not None:
                        norm_rest(e, chain, norm, g - 2)
                        e.sem_inc(sem("table_made"), 1)
            nodes(1, "gcn", "ndst", take_gcn, 2)
            sum_pass_vector(e, 2)
            nodes(2, "hop1", "inv", take_hop1, None)
            sum_pass_vector(e, 3)
            nodes(3, "hop2", "inv", take_add("hop2"), 3)
            e.wait_ge(sem("w_turned"), 1)
            chain(e.tensor_copy(w_last[:, :], pa[:, 0:D]))
            e.sem_inc(sem("w_copied"), 1)

            def body4(i):
                for r in range(R):
                    b = i * R + r
                    load_masks(e, loop_chain, i, r)
                    wait(e, f"first4_{r}", i * 48 + 48)
                    loop_chain(e.tensor_copy(srcf[:, :], idx[:, r, :]))
                    e.sem_inc(sem("numbered"), 1)
                    scan_columns(e, loop_chain, fill, b, r, mblk[:, 0, :], ALU.mult, ALU.add, range(K))
                    e.sem_inc(sem("filled4"), 1)
                    for q, cols in enumerate(LASTQ):
                        g = b * NL + q
                        wait(e, "spread", g + 1)
                        wait(e, "products4", b * NL + (q + 1 - back(q)))
                        wait(e, "matched", b * NL + (q + 1 - back(q)))
                        for k, j in enumerate(cols):
                            row = tp[q % 2][:, k * P:(k + 1) * P]
                            e.tensor_scalar(eqw[:, q % 2, k, :], row, srcf[:, j:j + 1], wblk[:, r, j:j + 1],
                                            ALU.is_equal, ALU.mult)
                            last = e.scalar_tensor_tensor(out=dupjunk[:, q % 2, k, :], in0=row, scalar=srcf[:, j:j + 1],
                                                          in1=earlier[:, :], op0=ALU.is_equal, op1=ALU.mult,
                                                          accum_out=dupc[:, j:j + 1])
                        last.then_inc(sem("matched"), 1)
                    wait(e, "matched", b * NL + NL)
                    loop_chain(e.tensor_scalar(dup1[:, :], dupc[:, :], 0.0, None, ALU.is_gt))
                    loop_chain(e.tensor_scalar(dup2[:, :], srcf[:, :], -1.0, spare[:, 0:1], ALU.mult, ALU.add))
                    loop_chain(e.tensor_tensor(dup2[:, :], dup2[:, :], dup1[:, :], ALU.mult))
                    wait_slot_added(e, i, r)
                    loop_chain(e.tensor_tensor(idx2[:, r, :], dup2[:, :], srcf[:, :], ALU.add))
                    loop_chain.clear()
                    e.sem_inc(sem("targets"), 1)
            loop(e, body4)
            for g in range(NGROUPS + 1):
                if g < NGROUPS:
                    m = M[:, g * NT:(g + 1) * NT, :]
                    e.wait_ge(sem(f"acc_in{g % 2}"), 16 * len(accs) * (g // 2 + 1))
                    copies = (ring if g % 2 else fill)[:, :, :, :].rearrange("p r k f -> p (r k) f")
                    chain(e.tensor_reduce(out=m, in_=copies[:, 0:len(accs) * NT, :].rearrange(
                        "p (k t) f -> p t f k", k=len(accs)), op=ALU.add, axis=AX.X))
                    e.sem_inc(sem("aggregated"), 1)
                if g:
                    mm_vector(e, "last", g - 1, D, take_add("last"))
            e.sem_inc(sem("x_final"), 1)

        @block.scalar
        def _(e):
            zero = fill[:, :, :, :].rearrange("p r k f -> p (r k) f")
            firsts = iter(range(0, LANE, R * K))

            def zero_part(c):
                e.dma_start(lrows(first_rows)[:, c:c + R * K, :], zero).then_inc(sem("zeroed"), 16)
            e.wait_ge(sem("fill_clear"), 1)
            e.wait_ge(sem("x_in"), 32)
            for _ in range(ZERO_FIRST):
                zero_part(next(firsts))
            for g in range(NGROUPS + 1):
                if g < NGROUPS:
                    norm_scalar(e, 0, g)
                    if g < ZERO_BETWEEN:
                        zero_part(next(firsts))
                if g:
                    mm_scalar(e, "ab", g - 1, D)
            e.wait_ge(sem("tab0"), 16 * NGROUPS)
            for c in firsts:
                zero_part(c)
            e.wait_ge(sem("degrees"), 1)
            e.activation(stat["ndst"][:, :], stat["deg"][:, :], ACT.Sqrt).then_inc(sem("rooted"), 1)

            def body0(i):
                for r in range(R):
                    b = i * R + r
                    wait(e, "summed0", b + 1)
                    e.activation(ring[:, r, :, :], ring[:, r, :, :], ACT.Relu).then_inc(sem("relued0"), 1)
                    for q, cols in enumerate(MAXQ):
                        rows, w = (P, len(cols) // 2 * P) if len(cols) > 1 else (D, P)
                        wait(e, "turned0", b * NQ + (q + 1))
                        wait(e, "products0", b * NQ + (q - 1))
                        e.activation(hT[0:rows, q % 2, 0:w], tp[q % 2][0:rows, 0:w], ACT.Copy)\
                            .then_inc(sem("copied0"), 1)
                    pass_store(e, 0, i, r)
            loop(e, body0)
            e.wait_ge(sem("degrees"), 2)
            e.activation(stat["nsrc"][:, :], stat["nsrc"][:, :], ACT.Sqrt).then_inc(sem("rooted"), 1)
            for g in range(NGROUPS):
                norm_scalar(e, 1, g)
            for l, name, kd, norm in ((1, "gcn", D, 2), (2, "hop1", 2 * D, None), (3, "hop2", 2 * D, 3)):
                def body(i):
                    for r in range(R):
                        pass_store(e, l, i, r)
                loop(e, body)
                for g in range(NGROUPS):
                    mm_scalar(e, name, g, kd)
                    if norm is not None:
                        norm_scalar(e, norm, g)

            def body4(i):
                for r in range(R):
                    b = i * R + r
                    wait_slot_added(e, i, r)
                    for q, cols in enumerate(LASTQ):
                        wait(e, "products4", b * NL + (q + 1))
                        e.activation(ring[:, r, cols[0]:cols[-1] + 1, :],
                                     om[q % 2][:, 0:len(cols) * D].rearrange("p (k f) -> p k f", f=D), ACT.Copy)\
                            .then_inc(sem("messages"), 1)
            loop(e, body4)
            for g in range(NGROUPS):
                mm_scalar(e, "last", g, 2 * D)

        @block.tensor
        def _(e):
            e.wait_ge(sem("const"), 1)
            e.wait_ge(sem("checked"), 1)
            for c in range(2):
                last = e.matmul(pb[0:1, 0:1], bad[:, c:c + 1], ones[:, 0:1], start=c == 0, stop=c == 1)
            last.then_inc(sem("bad_counted"), 1)
            with unsorted(e):
                sort_tensor(e)
            count_tensor(e, "hd", 0, PGRP, True)
            e.wait_ge(sem("counted"), 1)
            e.matmul(pa[:, 0:1], before[:, :], col["tot"][:, :], start=True, stop=True)
            e.matmul(pb[0:D, :], col["k"][:, 0:1].broadcast_to([P, D]), ident[:, :], start=True, stop=True)\
                .then_inc(sem("offset"), 1)
            for g in range(NGROUPS):
                e.wait_ge(sem("normed"), g + 1)
                mm_tensor(e, "ab", g, 0, D, w_ab[:, :], 2 * D)
            e.wait_ge(sem("placeable"), 1)

            def turn(b, r, q):
                wait(e, "copied0", b * NQ + (q - 1))
                gate(e)
                for k, c in enumerate(pairs(MAXQ[q])):
                    m = len(c) * D
                    last = e.transpose(tp[q % 2][0:m, k * P:(k + 1) * P],
                                       ring[:, r, c[0]:c[-1] + 1, :], ident[:, :])
                last.then_inc(sem("turned0"), 1)

            def body0(i):
                for r in range(R):
                    b = i * R + r
                    wait(e, "relued0", b + 1)
                    turn(b, r, 0)
                    for q, cols in enumerate(MAXQ):
                        if q + 1 < NQ:
                            turn(b, r, q + 1)
                        wait(e, "copied0", b * NQ + (q + 1))
                        wait(e, "taken0", b * NQ + (q - 1))
                        for k, c in enumerate(pairs(cols)):
                            m = len(c) * D
                            last = e.matmul(om[q % 2][:, k * P:k * P + m], hT[0:m, q % 2, k * P:(k + 1) * P],
                                            w_diag[0:m, 0:m], start=True, stop=True)
                        last.then_inc(sem("products0"), 1)
                    count_tensor(e, "hs", b * (K // HG), K // HG, isinstance(i, int) and r == 0)
            loop(e, body0)
            fix_tensor(e, 0)
            for l, name, c0, rhs in ((1, "gcn", D, w_gcn), (2, "hop1", 0, w_hop1), (3, "hop2", 0, w_hop2)):
                fix_tensor(e, l)
                for g in range(NGROUPS):
                    e.wait_ge(sem("aggregated"), (l - 1) * NGROUPS + g + 1)
                    mm_tensor(e, name, g, c0, 2 * D, rhs[:, :], D)
            e.transpose(pa[:, 0:D], w_lastT[:, :], ident[0:D, 0:D]).then_inc(sem("w_turned"), 1)

            def spread(b, q, cols):
                wait(e, "matched", b * NL + (q + 1 - back(q)))
                for k, j in enumerate(cols):
                    last = e.matmul(tp[q % 2][:, k * P:(k + 1) * P], srcf[:, j:j + 1].broadcast_to([P, P]),
                                    ident[:, :], start=True, stop=True)
                last.then_inc(sem("spread"), 1)

            def body4(i):
                for r in range(R):
                    b = i * R + r
                    wait(e, "numbered", b + 1)
                    spread(b, 0, LASTQ[0])
                    for q, cols in enumerate(LASTQ):
                        if q + 1 < NL:
                            spread(b, q + 1, LASTQ[q + 1])
                        if q == 0:
                            wait(e, "filled4", b + 1)
                        wait(e, "matched", b * NL + (q + 1))
                        wait(e, "messages", b * NL + (q + 1 - back(q)))
                        for k, j in enumerate(cols):
                            last = e.matmul(om[q % 2][:, k * D:(k + 1) * D], eqw[:, q % 2, k, :],
                                            fill[:, r, j, :], start=True, stop=True)
                        last.then_inc(sem("products4"), 1)
            loop(e, body4)
            e.wait_ge(sem("w_copied"), 1)
            for g in range(NGROUPS):
                e.wait_ge(sem("aggregated"), 3 * NGROUPS + g + 1)
                mm_tensor(e, "last", g, 0, 2 * D, w_last[:, :], D)


_INS = ["x", "src", "dst", "edge_weight", "L0_gnn_W1", "L0_gnn_b1", "L0_gnn_W2", "L0_gnn_b2", "L1_gnn_W",
        "L1_gnn_b", "L2_gnn_W1", "L2_gnn_b1", "L2_gnn_W2", "L2_gnn_b2", "L3_gnn_W_self", "L3_gnn_b_self",
        "L3_gnn_W_neigh", "L3_gnn_b_neigh"]


def kernel(**inputs):
    import numpy as _np
    import concourse.bacc as _bacc
    from concourse import mybir as _mybir
    from concourse.bass_utils import run_bass_kernel_spmd as _run

    nc = _bacc.Bacc("TRN2", target_bir_lowering=False, num_devices=1)
    arrays, args = {}, []
    for name in _INS:
        a = _np.ascontiguousarray(inputs[name])
        arrays["in_" + name] = a
        args.append(nc.dram_tensor("in_" + name, a.shape, _mybir.dt.from_np(a.dtype), kind="ExternalInput").ap())
    args.append(nc.dram_tensor("out_0", (N, D), _mybir.dt.float32, kind="ExternalOutput").ap())
    build(nc, *args)
    return _run(nc, [arrays], core_ids=[0]).results[0]["out_0"]
```
